# Optimizing a Trainium2 kernel written in Bass

```python
import numpy as np
import jax
import jax.numpy as jnp

def _softmax(x, axis=-1):
    return jax.nn.softmax(x, axis=axis)

def _gelu(x):
    return jax.nn.gelu(x, approximate=True)

def _silu(x):
    return jax.nn.silu(x)

def _sigmoid(x):
    return jax.nn.sigmoid(x)

def _layernorm(x, axis=-1, eps=1e-05):
    m = jnp.mean(x, axis=axis, keepdims=True)
    v = jnp.var(x, axis=axis, keepdims=True)
    return (x - m) / jnp.sqrt(v + eps)

def _scatter_add(tgt, idx, src, axis=0):
    return tgt.at[idx].add(src)

def _segment_sum(src, seg, n):
    return jax.ops.segment_sum(src, seg, n)
kernel_name = 'mk_decoder_preln_d1_seqx_r4_d032a9'

def setup_inputs(seed: int=0):
    np.random.seed(seed)
    _w = jnp.asarray

    def _rec_inputs():
        import jax
        import jax.numpy as jnp
        _rk = jax.random.key(seed)
        x = -0.0002928 + 1 * jax.random.normal(jax.random.fold_in(_rk, 1), (16, 128, 256), jnp.float32)
        _lenS = 128 - jax.random.randint(jax.random.fold_in(_rk, 7), (16,), 0, max(1, 128 // 4) + 1, jnp.int32)
        _lenS2 = 128 - jax.random.randint(jax.random.fold_in(_rk, 8), (16,), 0, max(1, 128 // 4) + 1, jnp.int32)
        _ctx_1024P = jax.random.normal(jax.random.fold_in(_rk, 11), (16, 16, 256), jnp.float32)
        _ctx_1024c = jax.random.dirichlet(jax.random.fold_in(_rk, 511), 0.3 * jnp.ones((16,), jnp.float32), (16, 128))
        _ctx_1024t = jnp.einsum('bsk,bkd->bsd', _ctx_1024c, _ctx_1024P)
        _ctx_1024t = _ctx_1024t * jax.lax.rsqrt(jnp.mean(jnp.square(_ctx_1024t)) + 1e-12) * 0.953939
        ctx_1024 = -1.39393e-06 + 0.999914 * (_ctx_1024t + 0.3 * jax.random.normal(jax.random.fold_in(_rk, 611), (16, 128, 256), jnp.float32))
        return (x, ctx_1024)
    x, ctx_1024 = _rec_inputs()

    def _L0_attn_setup():
        import jax, jax.numpy as jnp
        import numpy as np
        HIDDEN = 256
        HEADS = 8
        HEAD = HIDDEN // HEADS
        EPS = 1e-05

        def _gammas():
            lo = np.log(1.0 / 512.0)
            hi = np.log(1.0 / 32.0)
            lin = np.linspace(lo, hi, HEADS)
            return jnp.asarray(1.0 - np.exp(lin), dtype=jnp.float32)

        def _decay_mask(S, gammas):
            idx = jnp.arange(S)
            diff = idx[:, None] - idx[None, :]
            causal = diff >= 0
            safe = jnp.where(causal, diff, 0).astype(jnp.float32)
            D = jnp.where(causal[None], gammas[:, None, None] ** safe[None], 0.0)
            return D

        def _msr_forward(x, Wq, Wk, Wv, W1, W2, gn_w, gn_b):
            B, S, _ = x.shape
            xh = x.reshape(B, S, HEADS, HEAD)
            q = jnp.einsum('bshd,hde->bshe', xh, Wq)
            k = jnp.einsum('bshd,hde->bshe', xh, Wk)
            v = jnp.einsum('bshd,hde->bshe', xh, Wv)
            D = _decay_mask(S, _gammas())
            scores = jnp.einsum('bnhd,bmhd->bhnm', q, k) * D[None]
            ret = jnp.einsum('bhnm,bmhd->bnhd', scores, v)
            mu = jnp.mean(ret, axis=-1, keepdims=True)
            var = jnp.var(ret, axis=-1, keepdims=True)
            ret = (ret - mu) * jax.lax.rsqrt(var + EPS)
            ret = ret.reshape(B, S, HIDDEN) * gn_w + gn_b
            gated = x @ W1
            out = gated * jax.nn.sigmoid(gated) + ret
            return out @ W2
        key = jax.random.key(seed)
        ks = jax.random.split(key, 7)
        B, S = (2, 512)
        x = jax.random.normal(ks[0], (B, S, HIDDEN), dtype=jnp.float32)
        Wq = jax.random.normal(ks[1], (HEADS, HEAD, HEAD), dtype=jnp.float32) / HEAD
        Wk = jax.random.normal(ks[2], (HEADS, HEAD, HEAD), dtype=jnp.float32) / HEAD
        Wv = jax.random.normal(ks[3], (HEADS, HEAD, HEAD), dtype=jnp.float32) / HEAD
        W1 = jax.random.normal(ks[4], (HIDDEN, HIDDEN), dtype=jnp.float32) / HIDDEN
        W2 = jax.random.normal(ks[5], (HIDDEN, HIDDEN), dtype=jnp.float32) / HIDDEN
        gn_w = jnp.ones((HIDDEN,), dtype=jnp.float32)
        gn_b = jnp.zeros((HIDDEN,), dtype=jnp.float32)
        return {'x': x, 'Wq': Wq, 'Wk': Wk, 'Wv': Wv, 'W1': W1, 'W2': W2, 'gn_w': gn_w, 'gn_b': gn_b}
    _L0_attn_all = _L0_attn_setup()
    _L0_attn_in = {k: v for k, v in _L0_attn_all.items() if k in ('Wq', 'Wk', 'Wv', 'W1', 'W2', 'gn_w', 'gn_b')}
    del _L0_attn_all

    def _L0_xattn_setup():
        import jax, jax.numpy as jnp
        import numpy as np
        B, S, DIM, H = (2, 512, 256, 16)
        HD = DIM // H
        key = jax.random.key(seed)
        ks = jax.random.split(key, 11)
        sc = DIM ** (-0.5)
        return {'q': jax.random.normal(ks[0], (B, S, DIM), jnp.float32), 'k': jax.random.normal(ks[1], (B, S, DIM), jnp.float32), 'v': jax.random.normal(ks[2], (B, S, DIM), jnp.float32), 'Wq': jax.random.normal(ks[3], (DIM, DIM), jnp.float32) * sc, 'bq': jax.random.normal(ks[4], (DIM,), jnp.float32) * 0.02, 'Wk': jax.random.normal(ks[5], (DIM, DIM), jnp.float32) * sc, 'bk': jax.random.normal(ks[6], (DIM,), jnp.float32) * 0.02, 'Wv': jax.random.normal(ks[7], (DIM, DIM), jnp.float32) * sc, 'bv': jax.random.normal(ks[8], (DIM,), jnp.float32) * 0.02, 'Wo': jax.random.normal(ks[9], (DIM, DIM), jnp.float32) * sc, 'bo': jax.random.normal(ks[10], (DIM,), jnp.float32) * 0.02}
    _L0_xattn_all = _L0_xattn_setup()
    _L0_xattn_in = {k: v for k, v in _L0_xattn_all.items() if k in ('Wq', 'bq', 'Wk', 'bk', 'Wv', 'bv', 'Wo', 'bo')}
    del _L0_xattn_all

    def _L0_ffn_setup():
        import jax, jax.numpy as jnp
        import numpy as np
        NUM_EXPERTS = 8
        D_MODEL = 256
        D_FF = 1024
        BATCH, SEQ = (2, 1024)
        key = jax.random.key(seed)
        k_x, k_w1, k_w2 = jax.random.split(key, 3)
        x = jax.random.normal(k_x, (BATCH, SEQ, D_MODEL), dtype=jnp.float32)
        w1 = jax.random.normal(k_w1, (NUM_EXPERTS, D_MODEL, D_FF), dtype=jnp.float32) * (1.0 / np.sqrt(D_MODEL))
        b1 = jnp.zeros((NUM_EXPERTS, D_FF), dtype=jnp.float32)
        w2 = jax.random.normal(k_w2, (NUM_EXPERTS, D_FF, D_MODEL), dtype=jnp.float32) * (1.0 / np.sqrt(D_FF))
        b2 = jnp.zeros((NUM_EXPERTS, D_MODEL), dtype=jnp.float32)
        return {'x': x, 'w1': w1, 'b1': b1, 'w2': w2, 'b2': b2}
    _L0_ffn_all = _L0_ffn_setup()
    _L0_ffn_in = {k: v for k, v in _L0_ffn_all.items() if k in ('w1', 'b1', 'w2', 'b2')}
    del _L0_ffn_all
    return {'x': x, 'ctx_1024': ctx_1024, 'L0_attn_Wq': _L0_attn_in['Wq'], 'L0_attn_Wk': _L0_attn_in['Wk'], 'L0_attn_Wv': _L0_attn_in['Wv'], 'L0_attn_W1': _L0_attn_in['W1'], 'L0_attn_W2': _L0_attn_in['W2'], 'L0_attn_gn_w': _L0_attn_in['gn_w'], 'L0_attn_gn_b': _L0_attn_in['gn_b'], 'L0_xattn_Wq': _L0_xattn_in['Wq'], 'L0_xattn_bq': _L0_xattn_in['bq'], 'L0_xattn_Wk': _L0_xattn_in['Wk'], 'L0_xattn_bk': _L0_xattn_in['bk'], 'L0_xattn_Wv': _L0_xattn_in['Wv'], 'L0_xattn_bv': _L0_xattn_in['bv'], 'L0_xattn_Wo': _L0_xattn_in['Wo'], 'L0_xattn_bo': _L0_xattn_in['bo'], 'L0_ffn_w1': _L0_ffn_in['w1'], 'L0_ffn_b1': _L0_ffn_in['b1'], 'L0_ffn_w2': _L0_ffn_in['w2'], 'L0_ffn_b2': _L0_ffn_in['b2']}

def reference(x, ctx_1024, L0_attn_Wq, L0_attn_Wk, L0_attn_Wv, L0_attn_W1, L0_attn_W2, L0_attn_gn_w, L0_attn_gn_b, L0_xattn_Wq, L0_xattn_bq, L0_xattn_Wk, L0_xattn_bk, L0_xattn_Wv, L0_xattn_bv, L0_xattn_Wo, L0_xattn_bo, L0_ffn_w1, L0_ffn_b1, L0_ffn_w2, L0_ffn_b2):
    import jax
    import jax.numpy as jnp

    def _L0_attn_ref(x, Wq, Wk, Wv, W1, W2, gn_w, gn_b):
        import jax, jax.numpy as jnp
        import numpy as np
        HIDDEN = 256
        HEADS = 8
        HEAD = HIDDEN // HEADS
        EPS = 1e-05

        def _gammas():
            lo = np.log(1.0 / 512.0)
            hi = np.log(1.0 / 32.0)
            lin = np.linspace(lo, hi, HEADS)
            return jnp.asarray(1.0 - np.exp(lin), dtype=jnp.float32)

        def _decay_mask(S, gammas):
            idx = jnp.arange(S)
            diff = idx[:, None] - idx[None, :]
            causal = diff >= 0
            safe = jnp.where(causal, diff, 0).astype(jnp.float32)
            D = jnp.where(causal[None], gammas[:, None, None] ** safe[None], 0.0)
            return D

        def _msr_forward(x, Wq, Wk, Wv, W1, W2, gn_w, gn_b):
            B, S, _ = x.shape
            xh = x.reshape(B, S, HEADS, HEAD)
            q = jnp.einsum('bshd,hde->bshe', xh, Wq)
            k = jnp.einsum('bshd,hde->bshe', xh, Wk)
            v = jnp.einsum('bshd,hde->bshe', xh, Wv)
            D = _decay_mask(S, _gammas())
            scores = jnp.einsum('bnhd,bmhd->bhnm', q, k) * D[None]
            ret = jnp.einsum('bhnm,bmhd->bnhd', scores, v)
            mu = jnp.mean(ret, axis=-1, keepdims=True)
            var = jnp.var(ret, axis=-1, keepdims=True)
            ret = (ret - mu) * jax.lax.rsqrt(var + EPS)
            ret = ret.reshape(B, S, HIDDEN) * gn_w + gn_b
            gated = x @ W1
            out = gated * jax.nn.sigmoid(gated) + ret
            return out @ W2
        return _msr_forward(x, Wq, Wk, Wv, W1, W2, gn_w, gn_b)

    def _L0_xattn_ref(q, k, v, Wq, bq, Wk, bk, Wv, bv, Wo, bo):
        import jax, jax.numpy as jnp
        import numpy as np
        B, S, DIM, H = (2, 512, 256, 16)
        HD = DIM // H
        b, s, _ = q.shape
        qh = (q @ Wq + bq).reshape(b, s, H, HD).transpose(0, 2, 1, 3)
        kh = (k @ Wk + bk).reshape(b, s, H, HD).transpose(0, 2, 1, 3)
        vh = (v @ Wv + bv).reshape(b, s, H, HD).transpose(0, 2, 1, 3)
        scale = HD ** (-0.5)
        scores = jnp.einsum('bhqd,bhkd->bhqk', qh, kh) * scale
        causal = jnp.triu(jnp.ones((s, s), dtype=bool), k=1)
        scores = jnp.where(causal, -jnp.inf, scores)
        attn = jax.nn.softmax(scores, axis=-1)
        out = jnp.einsum('bhqk,bhkd->bhqd', attn, vh)
        out = out.transpose(0, 2, 1, 3).reshape(b, s, DIM)
        return out @ Wo + bo

    def _L0_ffn_ref(x, w1, b1, w2, b2):
        import jax, jax.numpy as jnp
        import numpy as np
        NUM_EXPERTS = 8
        D_MODEL = 256
        D_FF = 1024
        BATCH, SEQ = (2, 1024)
        B, S, D = x.shape
        E = w1.shape[0]
        T = B * S // E
        tokens = x.reshape(E, T, D)
        h = jnp.einsum('etd,edf->etf', tokens, w1) + b1[:, None, :]
        h = jax.nn.gelu(h)
        y = jnp.einsum('etf,efd->etd', h, w2) + b2[:, None, :]
        return y.reshape(B, S, D)
    x = x + _L0_attn_ref(_layernorm(x, axis=-1), L0_attn_Wq, L0_attn_Wk, L0_attn_Wv, L0_attn_W1, L0_attn_W2, L0_attn_gn_w, L0_attn_gn_b)
    x = x + _L0_xattn_ref(_layernorm(x, axis=-1), ctx_1024, ctx_1024, L0_xattn_Wq, L0_xattn_bq, L0_xattn_Wk, L0_xattn_bk, L0_xattn_Wv, L0_xattn_bv, L0_xattn_Wo, L0_xattn_bo)
    x = x + _L0_ffn_ref(_layernorm(x, axis=-1), L0_ffn_w1, L0_ffn_b1, L0_ffn_w2, L0_ffn_b2)
    return x

_drawn_inputs = setup_inputs


def setup_inputs(seed=0):
    import zlib

    import numpy as np

    out = dict(_drawn_inputs(seed))
    spreads = {'L0_attn_gn_w': (1.0, 0.6),
     'L0_attn_gn_b': (0.0, 0.8),
     'L0_ffn_b1': (0.0, 0.1),
     'L0_ffn_b2': (0.0, 0.1)}
    factors = {'L0_attn_W1': 30.778,
     'L0_xattn_bq': 8.0,
     'L0_xattn_bk': 64.0,
     'L0_xattn_bv': 3.485,
     'L0_xattn_bo': 3.216}
    for name, (base, spread) in spreads.items():
        noise = np.random.default_rng([zlib.crc32(name.encode()), seed]).standard_normal(out[name].shape)
        drawn = base * np.exp(spread * noise) if base else spread * noise
        out[name] = jnp.asarray(drawn.astype(out[name].dtype))
    for name, factor in factors.items():
        out[name] = (out[name] * factor).astype(out[name].dtype)
    return out
```

```python
from contextlib import ExitStack

import numpy as np

import concourse.bass as bass
from concourse import mybir
from concourse.alu_op_type import AluOpType as ALU

ACT = mybir.ActivationFunctionType
F32 = mybir.dt.float32
BF16 = mybir.dt.bfloat16
AX_X = mybir.AxisListType.X

P = 128
D = 256
C = D // P
NB = 2
T = NB * P
STEPS = 8
RH, RD = 8, 32
XH, XD = 16, 16
RJ = P // RD
XI = P // XD
G = 4
VP = 32
FF = 1024
FC = FF // P
UP = FC // 2
EPS = 1e-5
MASKED = 1e30
XSCALE = float(XD) ** -0.5
WA_LOADS = 10
WB_LOADS = 7


def decay_table():
    lin = np.linspace(np.log(1.0 / 512.0), np.log(1.0 / 32.0), RH)
    gammas = (1.0 - np.exp(lin)).astype(np.float32)
    diff = np.arange(P)[None, :] - np.arange(P)[:, None]
    powers = gammas.astype(np.float64)[None, :, None] ** np.maximum(diff, 0)[:, None, :]
    return np.where(diff[:, None, :] >= 0, powers, 0.0).astype(np.float32)



def decoder_kernel(nc, x, ctx_in, Wq, Wk, Wv, W1, W2, gn_w, gn_b, xWq, xbq, xWk, xbk, xWv, xbv, xWo, xbo,
                   w1, b1, w2, b2, decay, out):
    ctx = ExitStack()
    with ctx:
        def sb(name, shape, dt=F32):
            return ctx.enter_context(nc.sbuf_tensor(name, shape, dt))

        def bank(name):
            return ctx.enter_context(nc.psum_tensor(name, [P, 512], F32))

        def signal(name):
            return ctx.enter_context(nc.semaphore(name))

        ident = sb("ident", [P, P])
        ident_bf = sb("ident_bf", [P, P], BF16)
        mask_bf = sb("mask_bf", [P, G, P], BF16)
        decay_sb = sb("decay_sb", [P, RH, P])
        minus_half = sb("minus_half", [P, NB * RH])
        wq_c = sb("wq_c", [P, C, RD])
        wk_c = sb("wk_c", [P, C, RD])
        wv_c = sb("wv_c", [P, C, RD])
        wv_mean = sb("wv_mean", [P, C])
        wq_bd = sb("wq_bd", [P, C, P])
        wk_bd = sb("wk_bd", [P, C, P])
        wv_bd = sb("wv_bd", [P, C, P])
        wqT_bd = sb("wqT_bd", [P, C, P])
        wkT_bd = sb("wkT_bd", [P, C, P])
        qk_bd = sb("qk_bd", [P, C, P])
        W1_sb = sb("W1_sb", [P, C, D])
        W2_sb = sb("W2_sb", [P, C, D])
        gn_sb = sb("gn_sb", [P, 2, C])
        xWq_sb = sb("xWq_sb", [P, C, D])
        xWk_sb = sb("xWk_sb", [P, C, D])
        xWv_sb = sb("xWv_sb", [P, C, D])
        xWo_sb = sb("xWo_sb", [P, C, D])
        xb_sb = sb("xb_sb", [P, 2, C])
        nbq = sb("nbq", [P, C])
        xbv_sb = sb("xbv_sb", [P, D])
        xbo_sb = sb("xbo_sb", [P, D])
        b1_rows = sb("b1_rows", [STEPS * FC, P])
        b1T = sb("b1T", [P, STEPS * FC])

        x_in = sb("x_in", [P, NB, D])
        x_keep = sb("x_keep", [P, NB, D])
        statA = sb("statA", [P, NB, 6])
        mvA = sb("mvA", [P, NB, 2])
        rsA = sb("rsA", [P, NB])
        xnA = sb("xnA", [P, NB, D])
        xTA = sb("xTA", [P, C, T])
        qTA = sb("qTA", [P, C * T])
        q_bd = sb("q_bd", [P, RJ, C * T])
        thA = sb("thA", [P, C, T])
        silA = sb("silA", [P, C, T])
        sgA = sb("sgA", [P, C, T])
        vA = sb("vA", [P, NB, D])
        scD = sb("scD", [P, NB, C, RJ, P])
        retT = sb("retT", [P, C, NB, P])
        sqA = sb("sqA", [P, NB * RH, RD])
        varA = sb("varA", [P, NB * RH])
        rstA = sb("rstA", [P, NB * RH])
        rnA = sb("rnA", [P, NB * RH, RD])
        outT = sb("outT", [P, C, T])
        x1 = sb("x1", [P, NB, D])

        c_in = sb("c_in", [P, NB, D])
        x1b = sb("x1b", [P, NB, D])
        statB = sb("statB", [P, NB, 6])
        mvB = sb("mvB", [P, NB, 2])
        rsB = sb("rsB", [P, NB])
        xnB = sb("xnB", [P, NB, D])
        xTB = sb("xTB", [P, C, T])
        cTB = sb("cTB", [P, C, T])
        qTB = sb("qTB", [P, C, T])
        kTB = sb("kTB", [P, C * T])
        k_bd = sb("k_bd", [P, XI, C * T])
        v_pad = sb("v_pad", [P, NB, XH, VP])
        negmax = sb("negmax", [P, 2, G])
        prob = sb("prob", [P, 2, G, P])
        probT = sb("probT", [P, 2, G, P])
        pvT = sb("pvT", [P, 2, 512])
        rden = sb("rden", [P, NB, XH])
        att = sb("att", [P, NB, XH, XD])
        attT = sb("attT", [P, C, T])
        x2 = sb("x2", [P, NB, D])

        x2b = sb("x2b", [P, NB, D])
        statC = sb("statC", [P, NB, 6])
        mvC = sb("mvC", [P, NB, 2])
        rsC = sb("rsC", [P, NB])
        xnC = sb("xnC", [P, NB, D])
        xTC = sb("xTC", [P, C, T])
        w1_sb = sb("w1_sb", [P, C, FF])
        w2_sb = sb("w2_sb", [P, FC, D])
        b1_cur = sb("b1_cur", [P, FC])
        b2_cur = sb("b2_cur", [P, D])
        hT = sb("hT", [P, FC, T])
        y_out = sb("y_out", [P, NB, D])

        a0, a1, b0, b1k, b2k, b3, c0, c1 = [bank(n) for n in ("a0", "a1", "b0", "b1k", "b2k", "b3", "c0", "c1")]

        SC_BANK = [a0, a1, a0, a1]
        S_BANK = [b2k, b0, b2k, b1k, b0, b2k, b2k, b1k]
        T_BANK = [b1k, b0, b2k, b1k, b0, b0, b2k, b0]
        K_BANK = [b1k, b1k]

        s_wA = signal("s_wA")
        s_wB = signal("s_wB")
        s_nbq = signal("s_nbq")
        s_b1T = signal("s_b1T")
        s_zero = signal("s_zero")
        s_apart = {nc.vector.engine: ctx.enter_context(nc.semaphore("s_apart_dve")),
                   nc.gpsimd.engine: ctx.enter_context(nc.semaphore("s_apart_pool"))}
        s_const = signal("s_const")
        s_cent = signal("s_cent")
        s_bd = signal("s_bd")
        s_setT = signal("s_setT")
        s_setC = signal("s_setC")
        s_qk = signal("s_qk")
        s_x = signal("s_x")
        s_lnA = signal("s_lnA")
        s_rsA = signal("s_rsA")
        s_xnA = signal("s_xnA")
        s_keep = signal("s_keep")
        s_TA = signal("s_TA")
        s_xTA = signal("s_xTA")
        s_qA = signal("s_qA")
        s_qTA = signal("s_qTA")
        s_qbd = signal("s_qbd")
        s_gA = signal("s_gA")
        s_thA = signal("s_thA")
        s_silh = signal("s_silh")
        s_silA = signal("s_silA")
        s_sgA = signal("s_sgA")
        s_vAp = signal("s_vAp")
        s_vA = signal("s_vA")
        s_scA = signal("s_scA")
        s_scD = signal("s_scD")
        s_ret = signal("s_ret")
        s_retT = signal("s_retT")
        s_rtok = signal("s_rtok")
        s_sqA = signal("s_sqA")
        s_varA = signal("s_varA")
        s_rstA = signal("s_rstA")
        s_rnA = signal("s_rnA")
        s_rnT = signal("s_rnT")
        s_outT = signal("s_outT")
        s_yA = signal("s_yA")
        s_x1 = signal("s_x1")

        s_c = signal("s_c")
        s_lnB = signal("s_lnB")
        s_rsB = signal("s_rsB")
        s_xnB = signal("s_xnB")
        s_x1b = signal("s_x1b")
        s_TxB = signal("s_TxB")
        s_TcB = signal("s_TcB")
        s_xTB = signal("s_xTB")
        s_cTB = signal("s_cTB")
        s_qB = signal("s_qB")
        s_qTB = signal("s_qTB")
        s_kB = signal("s_kB")
        s_kTB = signal("s_kTB")
        s_kbd = signal("s_kbd")
        s_vB = signal("s_vB")
        s_vpad = signal("s_vpad")
        s_S = signal("s_S")
        s_max = signal("s_max")
        s_prob = signal("s_prob")
        s_T = signal("s_T")
        s_pTa = signal("s_pTa")
        s_pTd = signal("s_pTd")
        s_pv = signal("s_pv")
        s_pvT = signal("s_pvT")
        s_K = signal("s_K")
        s_rden = signal("s_rden")
        s_att = signal("s_att")
        s_aT = signal("s_aT")
        s_attT = signal("s_attT")
        s_yB = signal("s_yB")
        s_x2 = signal("s_x2")

        s_w1 = signal("s_w1")
        s_w2 = signal("s_w2")
        s_b2 = signal("s_b2")
        s_b1c = signal("s_b1c")
        s_lnC = signal("s_lnC")
        s_rsC = signal("s_rsC")
        s_xnC = signal("s_xnC")
        s_x2b = signal("s_x2b")
        s_TC = signal("s_TC")
        s_xTC = signal("s_xTC")
        s_up = signal("s_up")
        s_hT = signal("s_hT")
        s_yC = signal("s_yC")
        s_yout = signal("s_yout")
        s_out = signal("s_out")

        x_v = x.rearrange("(s b) n d -> s n b d", b=NB)
        c_v = ctx_in.rearrange("(s b) n d -> s n b d", b=NB)
        out_v = out.rearrange("(s b) n d -> s n b d", b=NB)
        w1_v = w1.rearrange("e (c p) f -> e p c f", p=P)
        w2_v = w2.rearrange("e (c p) d -> e p c d", p=P)
        b1_v = b1.rearrange("e (f p) -> (e f) p", p=P)

        def chunked(w):
            return w.rearrange("(c p) n -> p c n", p=P)

        def heads(w):
            return w.rearrange("(c j) d e -> (j d) c e", c=C)

        def later(step):
            return not isinstance(step, int) or step > 0

        def wait_apart(eng):
            eng.sem_inc(s_apart[eng.engine], 1)

        def pipeline(eng, body):
            body(0, True, False, False, True)
            body(1, True, True, False, True)
            with eng.Fori(2, STEPS - 1) as i:
                body(i, True, True, True, True)
            body(STEPS - 1, True, True, True, False)
            body(STEPS, False, True, True, False)
            body(STEPS + 1, False, False, True, False)

        block = ctx.enter_context(nc.Block())

        @block.sync
        def _(sp):
            sp.dma_start(x_in[:, :, :], x_v[0]).then_inc(s_x, 16)
            for dst, src in ((wq_c, Wq), (wk_c, Wk), (wv_c, Wv)):
                sp.dma_start(dst[:, :, :], heads(src)).then_inc(s_wA, 16)
            sp.dma_start(W1_sb[:, :, :], chunked(W1)).then_inc(s_wA, 16)
            sp.dma_start(decay_sb[:, :, :], decay).then_inc(s_wA, 16)
            sp.dma_start(W2_sb[:, :, :], chunked(W2)).then_inc(s_wA, 16)
            with nc.allow_non_contiguous_dma(reason="four short vectors, once"):
                for dst, src in ((gn_sb[:, 0, :], gn_w), (gn_sb[:, 1, :], gn_b),
                                 (xb_sb[:, 0, :], xbq), (xb_sb[:, 1, :], xbk)):
                    sp.dma_start(dst, src.rearrange("(c p) -> p c", p=P)).then_inc(s_wA, 16)
            sp.dma_start(c_in[:, :, :], c_v[0]).then_inc(s_c, 16)
            for dst, src in ((xWq_sb, xWq), (xWk_sb, xWk), (xWv_sb, xWv), (xWo_sb, xWo)):
                sp.dma_start(dst[:, :, :], chunked(src)).then_inc(s_wB, 16)
            for dst, src in ((xbv_sb, xbv), (xbo_sb, xbo)):
                sp.dma_start(dst[:, :], src.partition_broadcast(P)).then_inc(s_wB, 16)
            sp.dma_start(b1_rows[:, :], b1_v).then_inc(s_wB, 16)
            sp.dma_start(b2_cur[:, :], b2[0].partition_broadcast(P)).then_inc(s_b2, 16)
            sp.dma_start(w1_sb[:, :, :], w1_v[0]).then_inc(s_w1, 16)
            sp.dma_start(w2_sb[:, :, :], w2_v[0]).then_inc(s_w2, 16)
            sp.wait_ge(s_zero, 2)

            def body(i, do_a, do_b, do_c, nextA):
                a, b, c = i, i - 1, i - 2
                if do_a:
                    sp.wait_ge(s_qTA, a + 1)
                    for j in range(RJ):
                        rows = slice(RD * j, RD * (j + 1))
                        sp.dma_start(q_bd[rows, j, :], qTA[rows, :]).then_inc(s_qbd, 16)
                if do_b:
                    sp.wait_ge(s_kTB, 2 * (b + 1))
                    for h in range(XI):
                        rows = slice(XD * h, XD * (h + 1))
                        sp.dma_start(k_bd[rows, h, :], kTB[rows, :]).then_inc(s_kbd, 16)
                if nextA:
                    sp.wait_ge(s_xnA, 2 * (a + 1))
                    sp.wait_ge(s_keep, a + 1)
                    sp.dma_start(x_in[:, :, :], x_v[a + 1]).then_inc(s_x, 16)
                if do_a and do_b:
                    sp.wait_ge(s_TcB, b + 1)
                    sp.dma_start(c_in[:, :, :], c_v[a]).then_inc(s_c, 16)
                if do_b and do_c:
                    sp.wait_ge(s_up, UP * (c + 1))
                    sp.dma_start(w1_sb[:, :, :], w1_v[b]).then_inc(s_w1, 16)
                    sp.wait_ge(s_x2b, c + 1)
                    sp.dma_start(b2_cur[:, :], b2[b].partition_broadcast(P)).then_inc(s_b2, 16)
                    sp.wait_ge(s_yC, c + 1)
                    sp.dma_start(w2_sb[:, :, :], w2_v[b]).then_inc(s_w2, 16)
                if do_c:
                    sp.wait_ge(s_yout, c + 1)
                    sp.dma_start(out_v[c], y_out[:, :, :]).then_inc(s_out, 16)

            pipeline(sp, body)
            sp.wait_ge(s_out, 16 * (STEPS - 1) + 16)

        @block.gpsimd
        def _(pool):
            pool.memset(ident[:, :], 0.0).then_inc(s_const, 1)
            pool.memset(ident_bf[:, :], 0.0).then_inc(s_const, 1)
            pool.memset(mask_bf[:, :, :], 0.0).then_inc(s_const, 1)
            pool.wait_ge(s_const, 3)
            for m in (ident, ident_bf):
                pool.affine_select(out=m[:, :], in_=m[:, :], compare_op=ALU.not_equal, fill=1.0, base=0,
                                   pattern=[[-1, P]], channel_multiplier=1).then_inc(s_const, 1)
            pool.affine_select(out=mask_bf[:, :, :], in_=mask_bf[:, :, :], compare_op=ALU.is_ge, fill=MASKED,
                               base=0, pattern=[[0, G], [-1, P]], channel_multiplier=1)\
                .then_inc(s_const, 1)
            pool.memset(minus_half[:, :], -0.5).then_inc(s_const, 1)
            pool.memset(v_pad[:, :, :, XD:XD + 1], 1.0).then_inc(s_const, 1)
            pool.memset(v_pad[:, :, :, XD + 1:VP], 0.0).then_inc(s_const, 1)
            pool.wait_ge(s_const, 9)

            def rsqrt(step, out, in_, s_in, per_step, s_out, n):
                pool.wait_ge(s_in, per_step * (step + 1))
                pool.tensor_tensor(out, in_, minus_half[:, 0:n], ALU.pow).then_inc(s_out, 1)

            def body(i, do_a, do_b, do_c, nextA):
                a, b, c = i, i - 1, i - 2
                if do_c:
                    rsqrt(c, rsC[:, :], mvC[:, :, 1], s_lnC, 4, s_rsC, NB)
                if do_a:
                    if later(a):
                        pool.wait_ge(s_x1, a)
                    wait_apart(pool)
                    pool.tensor_copy(x_keep[:, :, :], x_in[:, :, :]).then_inc(s_keep, 1)
                if do_b:
                    if isinstance(i, int) and i == 1:
                        pool.wait_ge(s_wB, 16 * WB_LOADS)
                    pool.wait_ge(s_x1, b + 1)
                    if later(b):
                        pool.wait_ge(s_x2, b)
                    pool.tensor_tensor(x1b[:, :, :], x1[:, :, :],
                                       xbo_sb[:, :].unsqueeze(1).broadcast_to([P, NB, D]), ALU.add)\
                        .then_inc(s_x1b, 1)
                if do_c:
                    pool.wait_ge(s_b2, 16 * (c + 1))
                    pool.wait_ge(s_x2, c + 1)
                    if later(c):
                        pool.wait_ge(s_yout, c)
                    pool.tensor_tensor(x2b[:, :, :], x2[:, :, :],
                                       b2_cur[:, :].unsqueeze(1).broadcast_to([P, NB, D]), ALU.add)\
                        .then_inc(s_x2b, 1)
                if do_a:
                    pool.wait_ge(s_silA, a + 1)
                    if later(a):
                        pool.wait_ge(s_outT, 2 * a)
                    wait_apart(pool)
                    for c in range(C):
                        pool.tensor_scalar(sgA[:, c, :], silA[:, c, :], 0.5, gn_sb[:, 1, c:c + 1],
                                           ALU.mult, ALU.add).then_inc(s_sgA, 1)
                    rsqrt(a, rstA[:, :], varA[:, :], s_varA, 2, s_rstA, NB * RH)
                if nextA:
                    rsqrt(a + 1, rsA[:, :], mvA[:, :, 1], s_lnA, 4, s_rsA, NB)
                if do_a:
                    rsqrt(a, rsB[:, :], mvB[:, :, 1], s_lnB, 4, s_rsB, NB)

            rsqrt(0, rsA[:, :], mvA[:, :, 1], s_lnA, 4, s_rsA, NB)
            pipeline(pool, body)

        @block.scalar
        def _(act):
            def copy(out, in_, done):
                nc.scalar.activation(out, in_, ACT.Copy).then_inc(done, 1)

            def body(i, do_a, do_b, do_c, nextA):
                a, b, c = i, i - 1, i - 2
                def gelu(u, bank):
                    act.wait_ge(s_up, UP * c + u + 1)
                    if u == 0:
                        act.wait_ge(s_b1c, c + 1)
                        if later(c):
                            act.wait_ge(s_yC, c)
                    for k in range(2):
                        f = 2 * u + k
                        ins = nc.scalar.activation(hT[:, f, :], bank[:, k * T:(k + 1) * T],
                                                   ACT.Gelu_apprx_tanh, bias=b1_cur[:, f:f + 1])
                    ins.then_inc(s_hT, 1)

                if do_a:
                    act.wait_ge(s_TA, a + 1)
                    copy(xTA[:, :, :], a0[:, :].rearrange("p (c t) -> p c t", c=C), s_xTA)
                if do_b:
                    act.wait_ge(s_TxB, b + 1)
                    copy(xTB[:, :, :], b0[:, :].rearrange("p (c t) -> p c t", c=C), s_xTB)
                    act.wait_ge(s_TcB, b + 1)
                    copy(cTB[:, :, :], b1k[:, :].rearrange("p (c t) -> p c t", c=C), s_cTB)
                if do_a:
                    act.wait_ge(s_qA, a + 1)
                    if later(a):
                        act.wait_ge(s_qbd, 16 * RJ * a)
                    copy(qTA[:, :], a1[:, :], s_qTA)
                if do_b:
                    act.wait_ge(s_qB, b + 1)
                    for m in range(C):
                        nc.scalar.activation(qTB[:, m, :], b2k[:, m * T:(m + 1) * T], ACT.Identity,
                                             bias=nbq[:, m:m + 1], scale=-XSCALE).then_inc(s_qTB, 1)
                    act.wait_ge(s_kB, b + 1)
                    if later(b):
                        act.wait_ge(s_kbd, 16 * XI * b)
                    for m in range(C):
                        nc.scalar.activation(kTB[:, m * T:(m + 1) * T], b0[:, m * T:(m + 1) * T],
                                             ACT.Identity, bias=xb_sb[:, 1, m:m + 1]).then_inc(s_kTB, 1)
                if do_a:
                    act.wait_ge(s_gA, a + 1)
                    nc.scalar.activation(thA[:, :, :], a0[:, :].rearrange("p (c t) -> p c t", c=C),
                                         ACT.Tanh, scale=0.5).then_inc(s_thA, 1)
                if do_c:
                    act.wait_ge(s_TC, c + 1)
                    copy(xTC[:, :, :], c0[:, :].rearrange("p (c t) -> p c t", c=C), s_xTC)
                    gelu(0, c1)
                    gelu(1, c0)
                    gelu(2, c1)
                    gelu(3, c0)

                def exps(u):
                    act.wait_ge(s_max, 8 * b + u + 1)
                    if u >= 2 or later(b):
                        act.wait_ge(s_T, 8 * b + u - 1)
                    for g in range(G):
                        ins = nc.scalar.activation(prob[:, u % 2, g, :], S_BANK[u][:, g * P:(g + 1) * P],
                                                   ACT.Exp, bias=negmax[:, u % 2, g:g + 1], scale=-1.0)
                    ins.then_inc(s_prob, 1)

                def probT_even(u):
                    act.wait_ge(s_T, 8 * b + u + 1)
                    if u >= 2 or later(b):
                        act.wait_ge(s_pv, 8 * b + u - 1)
                    copy(probT[:, u % 2, :, :], T_BANK[u][:, :].rearrange("p (g n) -> p g n", g=G), s_pTa)

                def pv_out(seq):
                    act.wait_ge(s_pv, 8 * b + 4 * seq + 4)
                    if later(b):
                        act.wait_ge(s_K, 2 * (b - 1) + seq + 1)
                    copy(pvT[:, seq, :], b3[:, :], s_pvT)

                if do_b:
                    exps(0)
                    exps(1)
                    probT_even(0)
                if do_a:
                    act.wait_ge(s_ret, a + 1)
                    copy(retT[:, :, :, :], a0[:, :].rearrange("p (c b n) -> p c b n", c=C, b=NB), s_retT)
                if do_b:
                    exps(2)
                if do_a:
                    act.wait_ge(s_rtok, a + 1)
                    nc.scalar.activation(sqA[:, :, :], a1[:, :].rearrange("p (h e) -> p h e", e=RD),
                                         ACT.Square).then_inc(s_sqA, 1)
                if do_b:
                    exps(3)
                    probT_even(2)
                    exps(4)
                    exps(5)
                    pv_out(0)
                    probT_even(4)
                    exps(6)
                    exps(7)
                    probT_even(6)
                    pv_out(1)
                    act.wait_ge(s_aT, b + 1)
                    copy(attT[:, :, :], b2k[:, :].rearrange("p (c t) -> p c t", c=C), s_attT)

            act.wait_ge(s_nbq, 1)
            pipeline(act, body)

        @block.vector
        def _(dve):
            dve.wait_ge(s_wA, 16 * WA_LOADS)
            nc.vector.tensor_reduce(wv_mean[:, :], wv_c[:, :, :], AX_X, ALU.add).then_inc(s_cent, 1)
            dve.wait_ge(s_cent, 1)
            nc.vector.tensor_scalar(wv_mean[:, :], wv_mean[:, :], 1.0 / RD, None, ALU.mult).then_inc(s_cent, 1)
            dve.wait_ge(s_cent, 2)
            nc.vector.tensor_tensor(wv_c[:, :, :], wv_c[:, :, :], wv_mean[:, :].unsqueeze(2).broadcast_to([P, C, RD]),
                                    ALU.subtract).then_inc(s_cent, 1)
            for w in (wq_bd, wk_bd, wv_bd):
                nc.vector.memset(w[:, :, :], 0.0).then_inc(s_cent, 1)
            dve.wait_ge(s_cent, 6)
            for w, src in ((wq_bd, wq_c), (wk_bd, wk_c), (wv_bd, wv_c)):
                for j in range(RJ):
                    rows = slice(RD * j, RD * (j + 1))
                    nc.vector.tensor_copy(w[rows, :, rows], src[rows, :, :]).then_inc(s_bd, 1)
            nc.vector.tensor_scalar(nbq[:, :], xb_sb[:, 0, :], -XSCALE, None, ALU.mult).then_inc(s_nbq, 1)
            nc.vector.memset(q_bd[:, :, :], 0.0).then_inc(s_zero, 1)
            nc.vector.memset(k_bd[:, :, :], 0.0).then_inc(s_zero, 1)
            dve.wait_ge(s_setT, 1)
            nc.vector.tensor_copy(wqT_bd[:, :, :], a0[:, 0:D].rearrange("p (c n) -> p c n", c=C))
            nc.vector.tensor_copy(wkT_bd[:, :, :], a0[:, D:2 * D].rearrange("p (c n) -> p c n", c=C))\
                .then_inc(s_setC, 1)
            dve.wait_ge(s_qk, 1)
            nc.vector.tensor_copy(qk_bd[:, :, :], a1[:, 0:D].rearrange("p (c n) -> p c n", c=C))\
                .then_inc(s_setC, 1)
            dve.wait_ge(s_b1T, 1)
            nc.vector.tensor_copy(b1T[:, :], c0[:, 0:STEPS * FC]).then_inc(s_setC, 1)
            dve.wait_ge(s_setC, 3)

            def statistics(step, src, stat, mv, s_ln):
                for b in range(NB):
                    nc.vector.bn_stats(stat[:, b, :], src[:, b, :]).then_inc(s_ln, 1)
                dve.wait_ge(s_ln, 4 * step + 2)
                wait_apart(dve)
                for b in range(NB):
                    ins = nc.vector.bn_aggr(mv[:, b, :], stat[:, b, :])
                ins.then_inc(s_ln, 1)
                dve.wait_ge(s_ln, 4 * step + 3)
                nc.vector.tensor_scalar(mv[:, :, 1], mv[:, :, 1], EPS, None, ALU.add).then_inc(s_ln, 1)

            def normalise(step, src, mv, rs, xn, s_rs, s_xn, s_read):
                dve.wait_ge(s_rs, step + 1)
                if later(step):
                    dve.wait_ge(s_read, step)
                for b in range(NB):
                    nc.vector.tensor_scalar(xn[:, b, :], src[:, b, :], mv[:, b, 0:1], rs[:, b:b + 1],
                                            ALU.subtract, ALU.mult).then_inc(s_xn, 1)

            def body(i, do_a, do_b, do_c, nextA):
                a, b, c = i, i - 1, i - 2
                if do_c:
                    dve.wait_ge(s_x2, c + 1)
                    statistics(c, x2, statC, mvC, s_lnC)
                    normalise(c, x2, mvC, rsC, xnC, s_rsC, s_xnC, s_TC)
                if do_c:
                    if later(c):
                        dve.wait_ge(s_hT, UP * c)
                    b1_col = b1T[:, :].rearrange("p (e f) -> p e f", f=FC)
                    nc.vector.tensor_copy(b1_cur[:, :], b1_col[:, c, :]).then_inc(s_b1c, 1)
                if do_a:
                    dve.wait_ge(s_thA, a + 1)
                    if later(a):
                        dve.wait_ge(s_sgA, 2 * a)
                    nc.vector.scalar_tensor_tensor(out=silA[:, :, :], in0=a0[:, :].rearrange("p (c t) -> p c t", c=C),
                                                   scalar=0.0, in1=thA[:, :, :], op0=ALU.add, op1=ALU.mult)\
                        .then_inc(s_silh, 1)
                    dve.wait_ge(s_silh, a + 1)
                    nc.vector.tensor_tensor(silA[:, :, :], a0[:, :].rearrange("p (c t) -> p c t", c=C),
                                            silA[:, :, :], ALU.add).then_inc(s_silA, 1)
                    dve.wait_ge(s_vAp, a + 1)
                    if later(a):
                        dve.wait_ge(s_ret, a)
                    nc.vector.tensor_copy(vA[:, :, :], a1[:, :].rearrange("p (b d) -> p b d", b=NB))\
                        .then_inc(s_vA, 1)
                if do_b:
                    dve.wait_ge(s_vB, b + 1)
                    if later(b):
                        dve.wait_ge(s_pv, 8 * b)
                    nc.vector.tensor_tensor(
                        v_pad[:, :, :, 0:XD], b1k[:, :].rearrange("p (b h e) -> p b h e", b=NB, e=XD),
                        xbv_sb[:, :].rearrange("p (h e) -> p h e", e=XD).unsqueeze(1).broadcast_to([P, NB, XH, XD]),
                        ALU.add).then_inc(s_vpad, 1)

                def decay(u):
                    dve.wait_ge(s_scA, 4 * a + u + 1)
                    if later(a):
                        dve.wait_ge(s_ret, a)
                    bk, cc = u // C, u % C
                    nc.vector.tensor_tensor(scD[:, bk, cc, :, :], SC_BANK[u][:, :].rearrange("p (j n) -> p j n", j=RJ),
                                            decay_sb[:, RJ * cc:RJ * (cc + 1), :], ALU.mult).then_inc(s_scD, 1)

                def maxima(u):
                    dve.wait_ge(s_S, 8 * b + u + 1)
                    if u >= 2 or later(b):
                        dve.wait_ge(s_prob, 8 * b + u - 1)
                    nc.vector.tensor_reduce(negmax[:, u % 2, :], S_BANK[u][:, :].rearrange("p (g m) -> p g m", g=G),
                                            AX_X, ALU.min).then_inc(s_max, 1)

                def probT_odd(u):
                    dve.wait_ge(s_T, 8 * b + u + 1)
                    if u >= 2 or later(b):
                        dve.wait_ge(s_pv, 8 * b + u - 1)
                    nc.vector.tensor_copy(probT[:, u % 2, :, :],
                                          T_BANK[u][:, :].rearrange("p (g n) -> p g n", g=G)).then_inc(s_pTd, 1)

                def divide(seq):
                    dve.wait_ge(s_K, 2 * b + seq + 1)
                    if later(b):
                        dve.wait_ge(s_aT, b)
                    kv = K_BANK[seq][:, :].rearrange("p (h e) -> p h e", e=VP)
                    nc.vector.reciprocal(rden[:, seq, :], kv[:, :, XD]).then_inc(s_rden, 1)
                    dve.wait_ge(s_rden, 2 * b + seq + 1)
                    nc.vector.tensor_tensor(att[:, seq, :, :], kv[:, :, 0:XD],
                                            rden[:, seq, :].unsqueeze(2).broadcast_to([P, XH, XD]), ALU.mult)\
                        .then_inc(s_att, 1)

                if do_a:
                    decay(0)
                    decay(1)
                if do_b:
                    maxima(0)
                if do_a:
                    decay(2)
                if do_b:
                    maxima(1)
                if do_a:
                    decay(3)
                if do_b:
                    maxima(2)
                    probT_odd(1)
                if do_a:
                    dve.wait_ge(s_sqA, a + 1)
                    nc.vector.tensor_reduce(varA[:, :], sqA[:, :, :], AX_X, ALU.add).then_inc(s_varA, 1)
                    dve.wait_ge(s_varA, 2 * a + 1)
                    nc.vector.tensor_scalar(varA[:, :], varA[:, :], 1.0 / RD, EPS, ALU.mult, ALU.add)\
                        .then_inc(s_varA, 1)
                if do_b:
                    maxima(3)
                    maxima(4)
                    probT_odd(3)
                if do_a:
                    dve.wait_ge(s_rstA, a + 1)
                    if later(a):
                        dve.wait_ge(s_rnT, a)
                    nc.vector.tensor_tensor(rnA[:, :, :], a1[:, :].rearrange("p (h e) -> p h e", e=RD),
                                            rstA[:, :].unsqueeze(2).broadcast_to([P, NB * RH, RD]), ALU.mult)\
                        .then_inc(s_rnA, 1)
                if do_b:
                    maxima(5)
                    divide(0)
                if do_a:
                    dve.wait_ge(s_rnT, a + 1)
                    dve.wait_ge(s_sgA, 2 * (a + 1))
                    if later(a):
                        dve.wait_ge(s_yA, a)
                    for k in range(C):
                        nc.vector.scalar_tensor_tensor(out=outT[:, k, :], in0=a0[:, k * T:(k + 1) * T],
                                                       scalar=gn_sb[:, 0, k:k + 1], in1=sgA[:, k, :],
                                                       op0=ALU.mult, op1=ALU.add).then_inc(s_outT, 1)
                if do_b:
                    maxima(6)
                if do_a:
                    dve.wait_ge(s_yA, a + 1)
                    dve.wait_ge(s_keep, a + 1)
                    if do_b:
                        dve.wait_ge(s_x1b, b + 1)
                    nc.vector.tensor_tensor(x1[:, :, :], a1[:, :].rearrange("p (b d) -> p b d", b=NB),
                                            x_keep[:, :, :], ALU.add).then_inc(s_x1, 1)
                if do_b:
                    probT_odd(5)
                    maxima(7)
                if nextA:
                    dve.wait_ge(s_x, 16 * (a + 2))
                    statistics(a + 1, x_in, statA, mvA, s_lnA)
                if do_a:
                    dve.wait_ge(s_x1, a + 1)
                    statistics(a, x1, statB, mvB, s_lnB)
                if do_b:
                    probT_odd(7)
                if nextA:
                    normalise(a + 1, x_in, mvA, rsA, xnA, s_rsA, s_xnA, s_TA)
                if do_a:
                    normalise(a, x1, mvB, rsB, xnB, s_rsB, s_xnB, s_TxB)
                if do_b:
                    divide(1)
                if do_c:
                    dve.wait_ge(s_yC, c + 1)
                    dve.wait_ge(s_x2b, c + 1)
                    if later(c):
                        dve.wait_ge(s_out, 16 * c)
                    nc.vector.tensor_tensor(y_out[:, :, :], c1[:, :].rearrange("p (b d) -> p b d", b=NB),
                                            x2b[:, :, :], ALU.add).then_inc(s_yout, 1)
                if do_b:
                    dve.wait_ge(s_yB, b + 1)
                    dve.wait_ge(s_x1b, b + 1)
                    if do_c:
                        dve.wait_ge(s_x2b, c + 1)
                    nc.vector.tensor_tensor(x2[:, :, :], b0[:, :].rearrange("p (b d) -> p b d", b=NB),
                                            x1b[:, :, :], ALU.add).then_inc(s_x2, 1)

            dve.wait_ge(s_x, 16)
            statistics(0, x_in, statA, mvA, s_lnA)
            normalise(0, x_in, mvA, rsA, xnA, s_rsA, s_xnA, s_TA)
            pipeline(dve, body)

        @block.tensor
        def _(pe):
            def mm(out, lhsT, rhs, start=True, stop=True):
                return nc.tensor.matmul(out, lhsT, rhs, start=start, stop=stop)

            pe.wait_ge(s_const, 9)
            pe.wait_ge(s_bd, 3 * RJ)
            for n, w in enumerate((wq_bd, wk_bd)):
                for k in range(C):
                    ins = nc.tensor.transpose(a0[:, (C * n + k) * P:(C * n + k + 1) * P], w[:, k, :], ident[:, :])
            ins.then_inc(s_setT, 1)
            pe.wait_ge(s_setC, 1)
            for k in range(C):
                ins = mm(a1[:, k * P:(k + 1) * P], wqT_bd[:, k, :], wkT_bd[:, k, :])
            ins.then_inc(s_qk, 1)
            pe.wait_ge(s_wB, 16 * WB_LOADS)
            n = STEPS * FC
            nc.tensor.transpose(c0[:, 0:n], b1_rows[:, :], ident[0:n, 0:n]).then_inc(s_b1T, 1)
            pe.wait_ge(s_setC, 3)

            def transposes(out, src, done):
                for k in range(C):
                    for b in range(NB):
                        col = k * T + b * P
                        ins = nc.tensor.transpose(out[:, col:col + P], src[:, b, k * P:(k + 1) * P], ident[:, :])
                ins.then_inc(done, 1)

            def to_channels(out, w, xT, done):
                for m in range(C):
                    for k in range(C):
                        ins = mm(out[:, m * T:(m + 1) * T], w[:, k, m * P:(m + 1) * P], xT[:, k, :],
                                 start=(k == 0), stop=(k == C - 1))
                ins.then_inc(done, 1)

            def to_tokens(out, xT, w, done):
                for b in range(NB):
                    for k in range(C):
                        ins = mm(out[:, b * D:(b + 1) * D], xT[:, k, b * P:(b + 1) * P], w[:, k, :],
                                 start=(k == 0), stop=(k == C - 1))
                ins.then_inc(done, 1)

            def body(i, do_a, do_b, do_c, nextA):
                a, b, c = i, i - 1, i - 2

                def ret_scores(u):
                    bk, cc = u // C, u % C
                    if u == 0:
                        pe.wait_ge(s_silA, a + 1)
                        pe.wait_ge(s_qbd, 16 * RJ * (a + 1))
                    elif u == 1:
                        pe.wait_ge(s_vA, a + 1)
                    else:
                        if u >= 2 or later(a):
                            pe.wait_ge(s_scD, 4 * a + u - 1)
                    tok = slice(bk * P, (bk + 1) * P)
                    qv = q_bd[:, :, :].rearrange("p j (c b n) -> p j c b n", c=C, b=NB)
                    mm(SC_BANK[u][:, :].rearrange("p (j n) -> p j n", j=RJ), xTA[:, cc, tok], qv[:, :, cc, bk, :])\
                        .then_inc(s_scA, 1)

                def scores(u):
                    bk, g = u // 4, u % 4
                    cc, hh = g // 2, g % 2
                    if u == 0:
                        pe.wait_ge(s_qTB, 2 * (b + 1))
                        pe.wait_ge(s_kbd, 16 * XI * (b + 1))
                    mm(S_BANK[u][:, :], ident_bf[:, :], mask_bf[:, :, :].rearrange("p g m -> p (g m)"),
                       start=True, stop=False)
                    kv = k_bd[:, :, :].rearrange("p i (c b m) -> p i c b m", c=C, b=NB)
                    mm(S_BANK[u][:, :].rearrange("p (g m) -> p g m", g=G), qTB[:, cc, bk * P:(bk + 1) * P],
                       kv[:, G * hh:G * (hh + 1), cc, bk, :], start=False, stop=True).then_inc(s_S, 1)

                def prob_transposes(u):
                    pe.wait_ge(s_prob, 8 * b + u + 1)
                    for g in range(G):
                        ins = nc.tensor.transpose(T_BANK[u][:, g * P:(g + 1) * P], prob[:, u % 2, g, :], ident[:, :])
                    ins.then_inc(s_T, 1)

                def with_values(u):
                    bk, g = u // 4, u % 4
                    if u % 2:
                        pe.wait_ge(s_pTd, 4 * b + u // 2 + 1)
                    else:
                        pe.wait_ge(s_pTa, 4 * b + u // 2 + 1)
                    if u == 0:
                        pe.wait_ge(s_vpad, b + 1)
                        if later(b):
                            pe.wait_ge(s_pvT, 2 * b)
                    if u == 4:
                        pe.wait_ge(s_pvT, 2 * b + 1)
                    for h in range(G):
                        ins = mm(b3[VP * h:VP * (h + 1), g * P:(g + 1) * P], v_pad[:, bk, G * g + h, :],
                                 probT[:, u % 2, h, :])
                    ins.then_inc(s_pv, 1)

                def values_to_tokens(seq):
                    pe.wait_ge(s_pvT, 2 * b + seq + 1)
                    for g in range(4):
                        ins = nc.tensor.transpose(K_BANK[seq][:, g * P:(g + 1) * P], pvT[:, seq, g * P:(g + 1) * P],
                                                  ident[:, :])
                    ins.then_inc(s_K, 1)

                def up(u, bank):
                    for k2 in range(2):
                        f = 2 * u + k2
                        for k in range(C):
                            ins = mm(bank[:, k2 * T:(k2 + 1) * T], w1_sb[:, k, f * P:(f + 1) * P], xTC[:, k, :],
                                     start=(k == 0), stop=(k == C - 1))
                    ins.then_inc(s_up, 1)

                def down(quarter):
                    bk, half = quarter // 2, quarter % 2
                    for f in range(half * FC // 2, (half + 1) * FC // 2):
                        ins = mm(c1[:, bk * D:(bk + 1) * D], hT[:, f, bk * P:(bk + 1) * P], w2_sb[:, f, :],
                                 start=(f == 0), stop=(f == FC - 1))
                    if quarter == 3:
                        ins.then_inc(s_yC, 1)

                if do_a:
                    pe.wait_ge(s_xnA, 2 * (a + 1))
                    if later(a):
                        pe.wait_ge(s_outT, 2 * a)
                    transposes(a0, xnA, s_TA)
                if do_b:
                    pe.wait_ge(s_xnB, 2 * (b + 1))
                    if later(b):
                        pe.wait_ge(s_x2, b)
                    transposes(b0, xnB, s_TxB)
                    pe.wait_ge(s_c, 16 * (b + 1))
                    if later(b):
                        pe.wait_ge(s_att, 2 * b)
                    transposes(b1k, c_in, s_TcB)
                if do_a:
                    pe.wait_ge(s_xTA, a + 1)
                    if later(a):
                        pe.wait_ge(s_x1, a)
                    for k in range(C):
                        ins = mm(a1[:, k * T:(k + 1) * T], qk_bd[:, k, :], xTA[:, k, :])
                    ins.then_inc(s_qA, 1)
                if do_b:
                    pe.wait_ge(s_xTB, b + 1)
                    if later(b):
                        pe.wait_ge(s_attT, b)
                    to_channels(b2k, xWq_sb, xTB, s_qB)
                    pe.wait_ge(s_cTB, b + 1)
                    to_channels(b0, xWk_sb, cTB, s_kB)
                if do_a:
                    to_channels(a0, W1_sb, xTA, s_gA)
                if do_b:
                    to_tokens(b1k, cTB, xWv_sb, s_vB)
                if do_a:
                    pe.wait_ge(s_qTA, a + 1)
                    for bk in range(NB):
                        for k in range(C):
                            col = bk * D + k * P
                            ins = mm(a1[:, col:col + P], xTA[:, k, bk * P:(bk + 1) * P], wv_bd[:, k, :])
                    ins.then_inc(s_vAp, 1)
                if do_c:
                    pe.wait_ge(s_xnC, 2 * (c + 1))
                    if later(c):
                        pe.wait_ge(s_hT, UP * c)
                    transposes(c0, xnC, s_TC)
                if do_a:
                    ret_scores(0)
                if do_c:
                    pe.wait_ge(s_xTC, c + 1)
                    pe.wait_ge(s_w1, 16 * (c + 1))
                    if later(c):
                        pe.wait_ge(s_yout, c)
                    up(0, c1)
                    up(1, c0)
                if do_a:
                    ret_scores(1)
                    ret_scores(2)
                if do_c:
                    pe.wait_ge(s_hT, UP * c + 1)
                    up(2, c1)
                if do_a:
                    ret_scores(3)
                if do_c:
                    pe.wait_ge(s_hT, UP * c + 2)
                    up(3, c0)
                if do_b:
                    scores(0)
                    pe.wait_ge(s_kTB, 2 * (b + 1))
                    scores(1)
                if do_a:
                    pe.wait_ge(s_scD, 4 * (a + 1))
                    for cc in range(C):
                        for bk in range(NB):
                            for j in range(RJ):
                                h = RJ * cc + j
                                ins = mm(a0[RD * j:RD * (j + 1), cc * T + bk * P:cc * T + (bk + 1) * P],
                                         vA[:, bk, RD * h:RD * (h + 1)], scD[:, bk, cc, j, :])
                    ins.then_inc(s_ret, 1)
                if do_c:
                    pe.wait_ge(s_hT, UP * (c + 1))
                    pe.wait_ge(s_w2, 16 * (c + 1))
                    down(0)
                if do_b:
                    pe.wait_ge(s_vpad, b + 1)
                    prob_transposes(0)
                    pe.wait_ge(s_prob, 8 * b + 1)
                    scores(2)
                    pe.wait_ge(s_prob, 8 * b + 2)
                    prob_transposes(1)
                    with_values(0)
                if do_a:
                    pe.wait_ge(s_retT, a + 1)
                    for bk in range(NB):
                        for cc in range(C):
                            col = bk * D + cc * P
                            ins = nc.tensor.transpose(a1[:, col:col + P], retT[:, cc, bk, :], ident[:, :])
                    ins.then_inc(s_rtok, 1)
                if do_b:
                    pe.wait_ge(s_pTa, 4 * b + 1)
                    scores(3)
                    pe.wait_ge(s_prob, 8 * b + 3)
                    prob_transposes(2)
                    with_values(1)
                if do_c:
                    down(1)
                if do_b:
                    pe.wait_ge(s_pTd, 4 * b + 1)
                    scores(4)
                    pe.wait_ge(s_prob, 8 * b + 4)
                    prob_transposes(3)
                    with_values(2)
                if do_a:
                    pe.wait_ge(s_rnA, a + 1)
                    for k in range(C):
                        for bk in range(NB):
                            col = k * T + bk * P
                            src = rnA[:, :, :].rearrange("p (b h) e -> p b (h e)", b=NB)
                            ins = nc.tensor.transpose(a0[:, col:col + P], src[:, bk, k * P:(k + 1) * P], ident[:, :])
                    ins.then_inc(s_rnT, 1)
                if do_b:
                    pe.wait_ge(s_pTa, 4 * b + 2)
                    scores(5)
                    with_values(3)
                    pe.wait_ge(s_prob, 8 * b + 5)
                    prob_transposes(4)
                    pe.wait_ge(s_pTd, 4 * b + 2)
                    values_to_tokens(0)
                    pe.wait_ge(s_prob, 8 * b + 6)
                    scores(6)
                if do_a:
                    pe.wait_ge(s_outT, 2 * (a + 1))
                    to_tokens(a1, outT, W2_sb, s_yA)
                if do_b:
                    with_values(4)
                    prob_transposes(5)
                    pe.wait_ge(s_att, 2 * b + 1)
                    scores(7)
                    with_values(5)
                if do_c:
                    down(2)
                if do_b:
                    pe.wait_ge(s_prob, 8 * b + 7)
                    prob_transposes(6)
                    with_values(6)
                    pe.wait_ge(s_pTd, 4 * b + 3)
                    prob_transposes(7)
                if do_c:
                    down(3)
                if do_b:
                    with_values(7)
                    pe.wait_ge(s_prob, 8 * (b + 1))
                    values_to_tokens(1)
                    pe.wait_ge(s_att, 2 * (b + 1))
                    pe.wait_ge(s_pTa, 4 * (b + 1))
                    attv = att[:, :, :, :].rearrange("p b h e -> p b (h e)")
                    transposes(b2k, attv, s_aT)
                    pe.wait_ge(s_attT, b + 1)
                    pe.wait_ge(s_pTd, 4 * (b + 1))
                    to_tokens(b0, attT, xWo_sb, s_yB)

            pipeline(pe, body)


_INS = ['x', 'ctx_1024', 'L0_attn_Wq', 'L0_attn_Wk', 'L0_attn_Wv', 'L0_attn_W1', 'L0_attn_W2', 'L0_attn_gn_w',
        'L0_attn_gn_b', 'L0_xattn_Wq', 'L0_xattn_bq', 'L0_xattn_Wk', 'L0_xattn_bk', 'L0_xattn_Wv', 'L0_xattn_bv',
        'L0_xattn_Wo', 'L0_xattn_bo', 'L0_ffn_w1', 'L0_ffn_b1', 'L0_ffn_w2', 'L0_ffn_b2']


def kernel(**inputs):
    import concourse.bacc as bacc
    from concourse.bass_utils import run_bass_kernel_spmd

    nc = bacc.Bacc("TRN2", target_bir_lowering=False, num_devices=1)
    arrays, args = {}, []
    for name in _INS:
        arrays[f"in_{name}"] = np.ascontiguousarray(inputs[name])
    arrays["in_decay"] = decay_table()
    for name, a in arrays.items():
        args.append(nc.dram_tensor(name, a.shape, mybir.dt.from_np(a.dtype), kind="ExternalInput").ap())
    out = nc.dram_tensor("out", (STEPS * NB, P, D), F32, kind="ExternalOutput").ap()
    decoder_kernel(nc, *args, out)
    r = run_bass_kernel_spmd(nc, [arrays], core_ids=[0])
    return r.results[0]["out"]
```

```python
from contextlib import ExitStack

import numpy as np

import concourse.bass as bass
from concourse import mybir
from concourse.alu_op_type import AluOpType as ALU

ACT = mybir.ActivationFunctionType
F32 = mybir.dt.float32
F32R = mybir.dt.float32r
BF16 = mybir.dt.bfloat16
AX_X = mybir.AxisListType.X
AX_XY = mybir.AxisListType.XY

P = 128
D = 256
C = D // P
NB = 2
T = NB * P
STEPS = 8
RH, RD = 8, 32
XH, XD = 16, 16
RJ = P // RD
PR = P // (2 * XD)
G = 4
VP = 32
FF = 1024
FC = FF // P
UP = FC // 2
EPS = 1e-5
MASKED = 1e30
XSCALE = float(XD) ** -0.5
ONE = 16 * 3
TWO = 2 * ONE
WH_LOADS = 3
WA_LOADS = 7
WB_LOADS = 7


def decay_table():
    lin = np.linspace(np.log(1.0 / 512.0), np.log(1.0 / 32.0), RH)
    gammas = (1.0 - np.exp(lin)).astype(np.float32)
    diff = np.arange(P)[None, :] - np.arange(P)[:, None]
    powers = gammas.astype(np.float64)[None, :, None] ** np.maximum(diff, 0)[:, None, :]
    return np.where(diff[:, None, :] >= 0, powers, 0.0).astype(np.float32)



def decoder_kernel(nc, x, ctx_in, Wq, Wk, Wv, W1, W2, gn_w, gn_b, xWq, xbq, xWk, xbk, xWv, xbv, xWo, xbo,
                   w1, b1, w2, b2, decay, out):
    ctx = ExitStack()
    with ctx:
        def sb(name, shape, dt=F32):
            return ctx.enter_context(nc.sbuf_tensor(name, shape, dt))

        def bank(name):
            return ctx.enter_context(nc.psum_tensor(name, [P, 512], F32))

        def signal(name):
            return ctx.enter_context(nc.semaphore(name))

        ident = sb("ident", [P, P])
        ident_bf = sb("ident_bf", [P, P], BF16)
        mask_bf = sb("mask_bf", [P, G, P], BF16)
        decay_sb = sb("decay_sb", [P, RH, P])
        minus_half = sb("minus_half", [P, NB * RH])
        wq_c = sb("wq_c", [P, C, RD])
        wk_c = sb("wk_c", [P, C, RD])
        wv_c = sb("wv_c", [P, C, RD])
        wv_mean = sb("wv_mean", [P, C])
        wv_bd = sb("wv_bd", [P, C, P])
        qk_bd = sb("qk_bd", [P, C, P])
        W1_sb = sb("W1_sb", [P, C, D])
        W2_sb = sb("W2_sb", [P, C, D])
        gn_sb = sb("gn_sb", [P, 2, C])
        xWq_sb = sb("xWq_sb", [P, C, D])
        xWk_sb = sb("xWk_sb", [P, C, D])
        xWv_sb = sb("xWv_sb", [P, C, D])
        xWo_sb = sb("xWo_sb", [P, C, D])
        xb_sb = sb("xb_sb", [P, 2, C])
        nbq = sb("nbq", [P, C])
        spare = sb("spare", [P, 1])
        head_of = sb("head_of", [P, 2])
        xbv_sb = sb("xbv_sb", [P, D])
        xbo_sb = sb("xbo_sb", [P, D])
        b1_rows = sb("b1_rows", [STEPS * FC, P])
        b1T = sb("b1T", [P, STEPS * FC])

        x_in = sb("x_in", [P, NB, D])
        x_keep = sb("x_keep", [P, NB, D])
        statA = sb("statA", [P, NB, 6])
        mvA = sb("mvA", [P, NB, 2])
        rsA = sb("rsA", [P, NB])
        xnA = sb("xnA", [P, NB, D])
        xTA = sb("xTA", [P, C, T])
        q_bd = sb("q_bd", [P, RJ, C * T])
        thA = sb("thA", [P, C, T])
        silA = sb("silA", [P, C, T])
        sgA = sb("sgA", [P, C, T])
        vA = sb("vA", [P, NB, D])
        scD = sb("scD", [P, NB, C, RJ, P])
        retT = sb("retT", [P, C, NB, P])
        sqA = thA[:, :, :].rearrange("p c t -> p (c t)").rearrange("p (h e) -> p h e", e=RD)
        varA = sb("varA", [P, NB * RH])
        rstA = sb("rstA", [P, NB * RH])
        rnA = retT[:, :, :, :].rearrange("p c b n -> p (c b n)").rearrange("p (h e) -> p h e", e=RD)
        outT = sb("outT", [P, C, T])
        x1 = sb("x1", [P, NB, D])

        c_in = sb("c_in", [P, NB, D])
        x1b = sb("x1b", [P, NB, D])
        statB = sb("statB", [P, NB, 6])
        mvB = sb("mvB", [P, NB, 2])
        rsB = sb("rsB", [P, NB])
        xnB = sb("xnB", [P, NB, D])
        xTB = sb("xTB", [P, C, T])
        cTB = sb("cTB", [P, C, T])
        q_hi = sb("q_hi", [P, C, T], F32R)
        q_lo = sb("q_lo", [P, C, T], F32R)
        kTB = sb("kTB", [P, C, T])
        k_hi = sb("k_hi", [P, 2, C, T], F32R)
        k_lo = sb("k_lo", [P, 2, C, T], F32R)
        q_st = sb("q_st", [P, PR, C, T], F32R)
        k_st = sb("k_st", [P, PR, 2, C, T], F32R)
        v_pad = sb("v_pad", [P, NB, XH, VP])
        negmax = sb("negmax", [P, 2, G])
        prob = sb("prob", [P, 2, G, P])
        probT = sb("probT", [P, 2, G, P])
        pvT = sb("pvT", [P, 2, 512])
        rden = sb("rden", [P, NB, XH])
        att = sb("att", [P, NB, XH, XD])
        attT = sb("attT", [P, C, T])
        x2 = sb("x2", [P, NB, D])

        x2b = sb("x2b", [P, NB, D])
        statC = sb("statC", [P, NB, 6])
        mvC = sb("mvC", [P, NB, 2])
        rsC = sb("rsC", [P, NB])
        xnC = sb("xnC", [P, NB, D])
        xTC_hi = sb("xTC_hi", [P, C, T], F32R)
        xTC_lo = sb("xTC_lo", [P, C, T], F32R)
        w1_hi = sb("w1_hi", [P, C, FF], F32R)
        w1_lo = sb("w1_lo", [P, C, FF], F32R)
        w2_hi = sb("w2_hi", [P, FC, D], F32R)
        w2_lo = sb("w2_lo", [P, FC, D], F32R)
        w_in = sb("w_in", [P, C * FF])
        b1_cur = sb("b1_cur", [P, FC])
        b2_cur = sb("b2_cur", [P, D])
        h_hi = sb("h_hi", [P, FC, T], F32R)
        h_lo = sb("h_lo", [P, FC, T], F32R)
        h_in = sb("h_in", [P, 2, 2, T])
        y_out = sb("y_out", [P, NB, D])

        wq_bd, wk_bd, wqT_bd, wkT_bd = [scD[:, 0, n // 2, 2 * (n % 2):2 * (n % 2) + C, :] for n in range(4)]

        w1_in = w_in[:, :].rearrange("p (c f) -> p c f", c=C)
        w2_in = w_in[:, :].rearrange("p (f d) -> p f d", f=FC)

        a0, a1, b0, b1k, b2k, b3, c0, c1 = [bank(n) for n in ("a0", "a1", "b0", "b1k", "b2k", "b3", "c0", "c1")]

        SC_BANK = [a0, a1, a0, a1]
        S_BANK = [b2k, b0, c0, b2k, b0, c0, b2k, b0]
        GROUP = [0, 2, 1, 3]

        s_wH = signal("s_wH")
        s_wA = signal("s_wA")
        s_wB = signal("s_wB")
        s_nbq = signal("s_nbq")
        s_head = signal("s_head")
        s_xWq = signal("s_xWq")
        s_b1T = signal("s_b1T")
        s_zero = signal("s_zero")
        s_zerod = signal("s_zerod")
        s_apart = {nc.vector.engine: ctx.enter_context(nc.semaphore("s_apart_dve")),
                   nc.gpsimd.engine: ctx.enter_context(nc.semaphore("s_apart_pool"))}
        s_const = signal("s_const")
        s_cent = signal("s_cent")
        s_bd = signal("s_bd")
        s_setT = signal("s_setT")
        s_setC = signal("s_setC")
        s_qk = signal("s_qk")
        s_x = signal("s_x")
        s_lnA = signal("s_lnA")
        s_rsA = signal("s_rsA")
        s_xnA = signal("s_xnA")
        s_keep = signal("s_keep")
        s_TA = signal("s_TA")
        s_xTA = signal("s_xTA")
        s_qA = signal("s_qA")
        s_qbda = signal("s_qbda")
        s_qbdd = signal("s_qbdd")
        s_gA = signal("s_gA")
        s_thA = signal("s_thA")
        s_silh = signal("s_silh")
        s_silA = signal("s_silA")
        s_sgA = signal("s_sgA")
        s_vAp = signal("s_vAp")
        s_vA = signal("s_vA")
        s_scA = signal("s_scA")
        s_scD = signal("s_scD")
        s_ret = signal("s_ret")
        s_retT = signal("s_retT")
        s_rtok = signal("s_rtok")
        s_sqA = signal("s_sqA")
        s_varA = signal("s_varA")
        s_rstA = signal("s_rstA")
        s_rnA = signal("s_rnA")
        s_rnT = signal("s_rnT")
        s_outT = signal("s_outT")
        s_yA = signal("s_yA")
        s_x1 = signal("s_x1")

        s_c = signal("s_c")
        s_lnB = signal("s_lnB")
        s_rsB = signal("s_rsB")
        s_xnB = signal("s_xnB")
        s_x1b = signal("s_x1b")
        s_TxB = signal("s_TxB")
        s_TcB = signal("s_TcB")
        s_xTB = signal("s_xTB")
        s_cTB = signal("s_cTB")
        s_qB = signal("s_qB")
        s_qhi = signal("s_qhi")
        s_qlo = signal("s_qlo")
        s_q01 = signal("s_q01")
        s_q23 = signal("s_q23")
        s_kB = signal("s_kB")
        s_kTB = signal("s_kTB")
        s_khi = signal("s_khi")
        s_klo = signal("s_klo")
        s_k0 = signal("s_k0")
        s_k1 = signal("s_k1")
        s_k23 = signal("s_k23")
        s_vB = signal("s_vB")
        s_vpad = signal("s_vpad")
        s_S = signal("s_S")
        s_max = signal("s_max")
        s_prob = signal("s_prob")
        s_T = signal("s_T")
        s_pTa = signal("s_pTa")
        s_pTd = signal("s_pTd")
        s_pv = signal("s_pv")
        s_pvT = signal("s_pvT")
        s_K = signal("s_K")
        s_rden = signal("s_rden")
        s_att = signal("s_att")
        s_aT = signal("s_aT")
        s_attT = signal("s_attT")
        s_yB = signal("s_yB")
        s_x2 = signal("s_x2")

        s_w1 = signal("s_w1")
        s_w2 = signal("s_w2")
        s_b2 = signal("s_b2")
        s_b1c = signal("s_b1c")
        s_lnC = signal("s_lnC")
        s_rsC = signal("s_rsC")
        s_xnC = signal("s_xnC")
        s_x2b = signal("s_x2b")
        s_TC = signal("s_TC")
        s_xTC = signal("s_xTC")
        s_xTClo = signal("s_xTClo")
        s_w1hi = signal("s_w1hi")
        s_w1lo = signal("s_w1lo")
        s_w2hi = signal("s_w2hi")
        s_w2lo = signal("s_w2lo")
        s_up = signal("s_up")
        s_hT = signal("s_hT")
        s_hhi = signal("s_hhi")
        s_hlo = signal("s_hlo")
        s_yC = signal("s_yC")
        s_yout = signal("s_yout")
        s_out = signal("s_out")

        x_v = x.rearrange("(s b) n d -> s n b d", b=NB)
        c_v = ctx_in.rearrange("(s b) n d -> s n b d", b=NB)
        out_v = out.rearrange("(s b) n d -> s n b d", b=NB)
        w1_v = w1.rearrange("e (c p) f -> e p c f", p=P)
        w2_v = w2.rearrange("e (c p) d -> e p c d", p=P)
        b1_v = b1.rearrange("e (f p) -> (e f) p", p=P)

        def chunked(w):
            return w.rearrange("(c p) n -> p c n", p=P)

        def heads(w):
            return w.rearrange("(c j) d e -> (j d) c e", c=C)

        def later(step):
            return not isinstance(step, int) or step > 0

        def wait_apart(eng):
            eng.sem_inc(s_apart[eng.engine], 1)

        def pipeline(eng, body):
            body(0, True, False, False, True)
            body(1, True, True, False, True)
            with eng.Fori(2, STEPS - 1) as i:
                body(i, True, True, True, True)
            body(STEPS - 1, True, True, True, False)
            body(STEPS, False, True, True, False)
            body(STEPS + 1, False, False, True, False)

        def stack_k(eng, r, done):
            rows = slice(2 * XD * r, 2 * XD * (r + 1))
            for part, src in enumerate((k_hi, k_lo, k_hi)):
                to = slice(2 * XD * part, 2 * XD * (part + 1))
                eng.dma_start(k_st[to, r, :, :, :].bitcast(F32), src[rows, :, :, :].bitcast(F32))\
                    .then_inc(done, 16)

        block = ctx.enter_context(nc.Block())

        @block.sync
        def _(sp):
            sp.dma_start(x_in[:, :, :], x_v[0]).then_inc(s_x, 16)
            for dst, src in ((wq_c, Wq), (wk_c, Wk), (wv_c, Wv)):
                sp.dma_start(dst[:, :, :], heads(src)).then_inc(s_wH, 16)
            sp.dma_start(W1_sb[:, :, :], chunked(W1)).then_inc(s_wA, 16)
            sp.dma_start(decay_sb[:, :, :], decay).then_inc(s_wA, 16)
            sp.dma_start(W2_sb[:, :, :], chunked(W2)).then_inc(s_wA, 16)
            with nc.allow_non_contiguous_dma(reason="four short vectors, once"):
                for dst, src in ((gn_sb[:, 0, :], gn_w), (gn_sb[:, 1, :], gn_b),
                                 (xb_sb[:, 0, :], xbq), (xb_sb[:, 1, :], xbk)):
                    sp.dma_start(dst, src.rearrange("(c p) -> p c", p=P)).then_inc(s_wA, 16)
            sp.dma_start(c_in[:, :, :], c_v[0]).then_inc(s_c, 16)
            for dst, src in ((xWq_sb, xWq), (xWk_sb, xWk), (xWv_sb, xWv), (xWo_sb, xWo)):
                sp.dma_start(dst[:, :, :], chunked(src)).then_inc(s_wB, 16)
            for dst, src in ((xbv_sb, xbv), (xbo_sb, xbo)):
                sp.dma_start(dst[:, :], src.partition_broadcast(P)).then_inc(s_wB, 16)
            sp.dma_start(b1_rows[:, :], b1_v).then_inc(s_wB, 16)
            sp.dma_start(b2_cur[:, :], b2[0].partition_broadcast(P)).then_inc(s_b2, 16)
            sp.dma_start(w1_in, w1_v[0]).then_inc(s_w1, 16)
            sp.wait_ge(s_zero, 2)

            def body(i, do_a, do_b, do_c, nextA):
                a, b, c = i, i - 1, i - 2
                if do_b:
                    sp.wait_ge(s_khi, 2 * (b + 1))
                    sp.wait_ge(s_klo, 2 * (b + 1))
                    stack_k(sp, 0, s_k0)
                if do_b:
                    sp.wait_ge(s_qhi, 2 * (b + 1))
                    for pairs, done in (((0, 1), s_q01), ((2, 3), s_q23)):
                        for part, src in enumerate((q_hi, q_hi, q_lo)):
                            if part == 2 and pairs == (0, 1):
                                sp.wait_ge(s_qlo, 2 * (b + 1))
                            for r in pairs:
                                rows = slice(2 * XD * r, 2 * XD * (r + 1))
                                to = slice(2 * XD * part, 2 * XD * (part + 1))
                                sp.dma_start(q_st[to, r, :, :].bitcast(F32), src[rows, :, :].bitcast(F32))\
                                    .then_inc(done, 16)
                if do_a and do_b:
                    sp.wait_ge(s_TcB, b + 1)
                    sp.dma_start(c_in[:, :, :], c_v[a]).then_inc(s_c, 16)
                if nextA:
                    sp.wait_ge(s_xnA, 2 * (a + 1))
                    sp.wait_ge(s_keep, a + 1)
                    sp.dma_start(x_in[:, :, :], x_v[a + 1]).then_inc(s_x, 16)
                if do_b and do_c:
                    sp.wait_ge(s_w2lo, UP * (c + 1))
                    sp.dma_start(w1_in, w1_v[b]).then_inc(s_w1, 16)
                    sp.wait_ge(s_x2b, c + 1)
                    sp.dma_start(b2_cur[:, :], b2[b].partition_broadcast(P)).then_inc(s_b2, 16)
                if do_b:
                    sp.wait_ge(s_w1lo, UP * (b + 1))
                    sp.dma_start(w2_in, w2_v[b]).then_inc(s_w2, 16)
                if do_c:
                    sp.wait_ge(s_yout, c + 1)
                    sp.dma_start(out_v[c], y_out[:, :, :]).then_inc(s_out, 16)

            pipeline(sp, body)
            sp.wait_ge(s_out, 16 * (STEPS - 1) + 16)

        @block.gpsimd
        def _(pool):
            pool.memset(ident[:, :], 0.0).then_inc(s_const, 1)
            pool.memset(ident_bf[:, :], 0.0).then_inc(s_const, 1)
            pool.memset(mask_bf[:, :, :], 0.0).then_inc(s_const, 1)
            pool.wait_ge(s_const, 3)
            for m in (ident, ident_bf):
                pool.affine_select(out=m[:, :], in_=m[:, :], compare_op=ALU.not_equal, fill=1.0, base=0,
                                   pattern=[[-1, P]], channel_multiplier=1).then_inc(s_const, 1)
            pool.affine_select(out=mask_bf[:, :, :], in_=mask_bf[:, :, :], compare_op=ALU.is_ge, fill=MASKED,
                               base=0, pattern=[[0, G], [-1, P]], channel_multiplier=1)\
                .then_inc(s_const, 1)
            pool.memset(minus_half[:, :], -0.5).then_inc(s_const, 1)
            pool.memset(v_pad[:, :, :, XD:XD + 1], 1.0).then_inc(s_const, 1)
            pool.memset(v_pad[:, :, :, XD + 1:VP], 0.0).then_inc(s_const, 1)
            pool.wait_ge(s_const, 9)

            def rsqrt(step, out, in_, s_in, per_step, s_out, n):
                pool.wait_ge(s_in, per_step * (step + 1))
                pool.tensor_tensor(out, in_, minus_half[:, 0:n], ALU.pow).then_inc(s_out, 1)

            def body(i, do_a, do_b, do_c, nextA):
                a, b, c = i, i - 1, i - 2
                if do_c:
                    rsqrt(c, rsC[:, :], mvC[:, :, 1], s_lnC, 4, s_rsC, NB)
                if do_b:
                    pool.wait_ge(s_khi, 2 * (b + 1))
                    pool.wait_ge(s_klo, 2 * (b + 1))
                    wait_apart(pool)
                    stack_k(pool, 1, s_k1)
                    stack_k(pool, 2, s_k23)
                    stack_k(pool, 3, s_k23)
                if do_c:
                    for u in range(UP):
                        part = slice(2 * u, 2 * (u + 1))
                        pool.wait_ge(s_w2hi, UP * c + u + 1)
                        pool.tensor_tensor(w2_lo[:, part, :], w2_in[:, part, :],
                                           w2_hi[:, part, :].bitcast(F32), ALU.subtract).then_inc(s_w2lo, 1)
                if do_a:
                    if later(a):
                        pool.wait_ge(s_x1, a)
                    wait_apart(pool)
                    pool.tensor_copy(x_keep[:, :, :], x_in[:, :, :]).then_inc(s_keep, 1)
                if do_b:
                    if isinstance(i, int) and i == 1:
                        pool.wait_ge(s_wB, 16 * WB_LOADS)
                    pool.wait_ge(s_x1, b + 1)
                    if later(b):
                        pool.wait_ge(s_x2, b)
                    pool.tensor_tensor(x1b[:, :, :], x1[:, :, :],
                                       xbo_sb[:, :].unsqueeze(1).broadcast_to([P, NB, D]), ALU.add)\
                        .then_inc(s_x1b, 1)
                if do_c:
                    pool.wait_ge(s_b2, 16 * (c + 1))
                    pool.wait_ge(s_x2, c + 1)
                    if later(c):
                        pool.wait_ge(s_yout, c)
                    pool.tensor_tensor(x2b[:, :, :], x2[:, :, :],
                                       b2_cur[:, :].unsqueeze(1).broadcast_to([P, NB, D]), ALU.add)\
                        .then_inc(s_x2b, 1)
                if do_a:
                    pool.wait_ge(s_silA, a + 1)
                    if later(a):
                        pool.wait_ge(s_outT, 2 * a)
                    wait_apart(pool)
                    for k in range(C):
                        pool.tensor_scalar(sgA[:, k, :], silA[:, k, :], 0.5, gn_sb[:, 1, k:k + 1],
                                           ALU.mult, ALU.add).then_inc(s_sgA, 1)
                if do_a:
                    rsqrt(a, rstA[:, :], varA[:, :], s_varA, 2, s_rstA, NB * RH)
                if do_b:
                    for u in range(UP):
                        part = slice(2 * P * u, 2 * P * (u + 1))
                        if u == 1 and nextA:
                            rsqrt(a + 1, rsA[:, :], mvA[:, :, 1], s_lnA, 4, s_rsA, NB)
                        pool.wait_ge(s_w1hi, UP * b + u + 1)
                        pool.tensor_tensor(w1_lo[:, :, part], w1_in[:, :, part],
                                           w1_hi[:, :, part].bitcast(F32), ALU.subtract).then_inc(s_w1lo, 1)
                elif nextA:
                    rsqrt(a + 1, rsA[:, :], mvA[:, :, 1], s_lnA, 4, s_rsA, NB)
                if do_a:
                    rsqrt(a, rsB[:, :], mvB[:, :, 1], s_lnB, 4, s_rsB, NB)

            rsqrt(0, rsA[:, :], mvA[:, :, 1], s_lnA, 4, s_rsA, NB)
            pool.memset(q_st[:, :, :, :].bitcast(F32), 0.0).then_inc(s_zero, 1)
            pool.memset(k_st[:, :, :, :, :].bitcast(F32), 0.0).then_inc(s_zero, 1)
            pool.wait_ge(s_zero, 2)
            pool.wait_ge(s_wB, 16 * WB_LOADS)
            pool.tensor_scalar(xWq_sb[:, :, :], xWq_sb[:, :, :], -XSCALE, None, ALU.mult).then_inc(s_xWq, 1)
            pipeline(pool, body)

        @block.scalar
        def _(act):
            def copy(out, in_, done):
                nc.scalar.activation(out, in_, ACT.Copy).then_inc(done, 1)

            def body(i, do_a, do_b, do_c, nextA):
                a, b, c = i, i - 1, i - 2
                def gelu(u, bank):
                    act.wait_ge(s_up, UP * c + u + 1)
                    if u == 0:
                        act.wait_ge(s_b1c, c + 1)
                    if u >= 2:
                        if u >= 2 or later(c):
                            act.wait_ge(s_hlo, UP * c + u - 1)
                    else:
                        if later(c):
                            act.wait_ge(s_hlo, UP * c)
                    for k in range(2):
                        f = 2 * u + k
                        ins = nc.scalar.activation(h_in[:, u % 2, k, :], bank[:, k * T:(k + 1) * T],
                                                   ACT.Gelu_apprx_tanh, bias=b1_cur[:, f:f + 1])
                    ins.then_inc(s_hT, 1)

                def round_w2(u):
                    part = slice(2 * u, 2 * (u + 1))
                    act.wait_ge(s_w2, 16 * (c + 1))
                    if later(c):
                        act.wait_ge(s_yC, c)
                    copy(w2_hi[:, part, :], w2_in[:, part, :], s_w2hi)

                def round_w1(u):
                    part = slice(2 * P * u, 2 * P * (u + 1))
                    act.wait_ge(s_w1, 16 * (b + 1))
                    if do_c:
                        act.wait_ge(s_up, UP * (c + 1))
                    copy(w1_hi[:, :, part], w1_in[:, :, part], s_w1hi)

                if do_a:
                    act.wait_ge(s_gA, a + 1)
                    nc.scalar.activation(thA[:, :, :], a0[:, :].rearrange("p (c t) -> p c t", c=C),
                                         ACT.Tanh, scale=0.5).then_inc(s_thA, 1)
                    act.wait_ge(s_qA, a + 1)
                    if later(a):
                        act.wait_ge(s_scA, 4 * a)
                    for j in (0, 1):
                        rows = slice(RD * j, RD * (j + 1))
                        copy(q_bd[rows, j, :], a1[rows, :], s_qbda)
                if do_b:
                    act.wait_ge(s_TxB, b + 1)
                    copy(xTB[:, :, :], b0[:, :].rearrange("p (c t) -> p c t", c=C), s_xTB)
                if do_c:
                    round_w2(0)
                    round_w2(1)
                    act.wait_ge(s_TC, c + 1)
                    copy(xTC_hi[:, :, :], c0[:, :].rearrange("p (c t) -> p c t", c=C), s_xTC)
                if do_b:
                    act.wait_ge(s_qB, b + 1)
                    if later(b):
                        act.wait_ge(s_q01, TWO * b)
                    if later(b):
                        act.wait_ge(s_q23, TWO * b)
                    for m in range(C):
                        nc.scalar.activation(q_hi[:, m, :], b0[:, m * T:(m + 1) * T], ACT.Identity,
                                             bias=nbq[:, m:m + 1]).then_inc(s_qhi, 1)
                if do_c:
                    gelu(0, c1)
                    round_w2(2)
                    gelu(1, c0)
                    round_w2(3)
                    gelu(2, c1)
                    gelu(3, c0)
                if do_b:
                    nc.scalar.activation(spare[:, :], minus_half[:, 0:1], ACT.Exp)

                def exps(u):
                    act.wait_ge(s_max, 8 * b + u + 1)
                    if u >= 2 or later(b):
                        act.wait_ge(s_T, 8 * b + u - 1)
                    for g in range(G):
                        ins = nc.scalar.activation(prob[:, u % 2, g, :], S_BANK[u][:, g * P:(g + 1) * P],
                                                   ACT.Exp, bias=negmax[:, u % 2, g:g + 1], scale=-1.0)
                    ins.then_inc(s_prob, 1)

                def probT_even(u):
                    act.wait_ge(s_T, 8 * b + u + 1)
                    if u >= 2 or later(b):
                        act.wait_ge(s_pv, 8 * b + u - 1)
                    copy(probT[:, u % 2, :, :], b1k[:, :].rearrange("p (g n) -> p g n", g=G), s_pTa)

                def pv_out(seq):
                    act.wait_ge(s_pv, 8 * b + 4 * seq + 4)
                    if later(b):
                        act.wait_ge(s_K, 2 * (b - 1) + seq + 1)
                    copy(pvT[:, seq, :], b3[:, :], s_pvT)

                if do_b:
                    exps(0)
                if do_a:
                    act.wait_ge(s_ret, a + 1)
                    copy(retT[:, :, :, :], a0[:, :].rearrange("p (c b n) -> p c b n", c=C, b=NB), s_retT)
                if do_b:
                    exps(1)
                    probT_even(0)
                    exps(2)
                if do_a:
                    act.wait_ge(s_rtok, a + 1)
                    nc.scalar.activation(sqA[:, :, :], a1[:, :].rearrange("p (h e) -> p h e", e=RD),
                                         ACT.Square).then_inc(s_sqA, 1)
                if do_b:
                    exps(3)
                    probT_even(2)
                    exps(4)
                    exps(5)
                    pv_out(0)
                    probT_even(4)
                    round_w1(0)
                    round_w1(1)
                    exps(6)
                    round_w1(2)
                    exps(7)
                    round_w1(3)
                    probT_even(6)
                if nextA:
                    transposed_x(a + 1)
                if do_b:
                    pv_out(1)
                if do_a:
                    act.wait_ge(s_TcB, a + 1)
                    copy(cTB[:, :, :], b1k[:, :].rearrange("p (c t) -> p c t", c=C), s_cTB)
                if do_b:
                    act.wait_ge(s_aT, b + 1)
                    copy(attT[:, :, :], b2k[:, :].rearrange("p (c t) -> p c t", c=C), s_attT)
                if do_a:
                    act.wait_ge(s_kB, a + 1)
                    if later(a):
                        act.wait_ge(s_klo, 2 * a)
                    for m in range(C):
                        nc.scalar.activation(kTB[:, m, :], a1[:, m * T:(m + 1) * T],
                                             ACT.Identity, bias=xb_sb[:, 1, m:m + 1]).then_inc(s_kTB, 1)

            def transposed_x(step):
                act.wait_ge(s_TA, step + 1)
                copy(xTA[:, :, :], a0[:, :].rearrange("p (c t) -> p c t", c=C), s_xTA)

            transposed_x(0)
            act.wait_ge(s_nbq, 1)
            act.wait_ge(s_const, 9)
            act.wait_ge(s_zerod, 1)
            pipeline(act, body)

        @block.vector
        def _(dve):
            def statistics(step, src, stat, mv, s_ln):
                for b in range(NB):
                    nc.vector.bn_stats(stat[:, b, :], src[:, b, :]).then_inc(s_ln, 1)
                dve.wait_ge(s_ln, 4 * step + 2)
                wait_apart(dve)
                for b in range(NB):
                    ins = nc.vector.bn_aggr(mv[:, b, :], stat[:, b, :])
                ins.then_inc(s_ln, 1)
                dve.wait_ge(s_ln, 4 * step + 3)
                nc.vector.tensor_scalar(mv[:, :, 1], mv[:, :, 1], EPS, None, ALU.add).then_inc(s_ln, 1)

            def normalise(step, src, mv, rs, xn, s_rs, s_xn, s_read):
                dve.wait_ge(s_rs, step + 1)
                if later(step):
                    dve.wait_ge(s_read, step)
                for b in range(NB):
                    nc.vector.tensor_scalar(xn[:, b, :], src[:, b, :], mv[:, b, 0:1], rs[:, b:b + 1],
                                            ALU.subtract, ALU.mult).then_inc(s_xn, 1)

            def body(i, do_a, do_b, do_c, nextA):
                a, b, c = i, i - 1, i - 2
                if do_c:
                    dve.wait_ge(s_x2, c + 1)
                    statistics(c, x2, statC, mvC, s_lnC)
                if do_a:
                    dve.wait_ge(s_qA, a + 1)
                    if later(a):
                        dve.wait_ge(s_scA, 4 * a)
                    for j in (2, 3):
                        rows = slice(RD * j, RD * (j + 1))
                        nc.vector.tensor_copy(q_bd[rows, j, :], a1[rows, :]).then_inc(s_qbdd, 1)
                if do_c:
                    normalise(c, x2, mvC, rsC, xnC, s_rsC, s_xnC, s_TC)
                if do_b:
                    dve.wait_ge(s_khi, 2 * (b + 1))
                    for h in range(2):
                        nc.vector.scalar_tensor_tensor(out=k_lo[:, h, :, :], in0=kTB[:, :, :],
                                                       scalar=head_of[:, h:h + 1], in1=k_hi[:, h, :, :].bitcast(F32),
                                                       op0=ALU.mult, op1=ALU.subtract).then_inc(s_klo, 1)
                if do_c:
                    if later(c):
                        dve.wait_ge(s_hT, UP * c)
                    b1_col = b1T[:, :].rearrange("p (e f) -> p e f", f=FC)
                    nc.vector.tensor_copy(b1_cur[:, :], b1_col[:, c, :]).then_inc(s_b1c, 1)
                if do_c:
                    dve.wait_ge(s_xTC, c + 1)
                    nc.vector.tensor_tensor(xTC_lo[:, :, :], c0[:, :].rearrange("p (c t) -> p c t", c=C),
                                            xTC_hi[:, :, :].bitcast(F32), ALU.subtract).then_inc(s_xTClo, 1)
                if do_a:
                    dve.wait_ge(s_thA, a + 1)
                    if later(a):
                        dve.wait_ge(s_sgA, 2 * a)
                    nc.vector.scalar_tensor_tensor(out=silA[:, :, :], in0=a0[:, :].rearrange("p (c t) -> p c t", c=C),
                                                   scalar=0.0, in1=thA[:, :, :], op0=ALU.add, op1=ALU.mult)\
                        .then_inc(s_silh, 1)
                    dve.wait_ge(s_silh, a + 1)
                    nc.vector.tensor_tensor(silA[:, :, :], a0[:, :].rearrange("p (c t) -> p c t", c=C),
                                            silA[:, :, :], ALU.add).then_inc(s_silA, 1)
                if do_b:
                    dve.wait_ge(s_qhi, 2 * (b + 1))
                    if later(b):
                        dve.wait_ge(s_q01, TWO * b)
                    if later(b):
                        dve.wait_ge(s_q23, TWO * b)
                    for m in range(C):
                        nc.vector.scalar_tensor_tensor(out=q_lo[:, m, :], in0=b0[:, m * T:(m + 1) * T],
                                                       scalar=nbq[:, m:m + 1], in1=q_hi[:, m, :].bitcast(F32),
                                                       op0=ALU.add, op1=ALU.subtract).then_inc(s_qlo, 1)
                if do_a:
                    dve.wait_ge(s_vAp, a + 1)
                    if later(a):
                        dve.wait_ge(s_ret, a)
                    nc.vector.tensor_copy(vA[:, :, :], a1[:, :].rearrange("p (b d) -> p b d", b=NB))\
                        .then_inc(s_vA, 1)
                if do_b:
                    dve.wait_ge(s_vB, b + 1)
                    if later(b):
                        dve.wait_ge(s_pv, 8 * b)
                    nc.vector.tensor_tensor(
                        v_pad[:, :, :, 0:XD], b1k[:, :].rearrange("p (b h e) -> p b h e", b=NB, e=XD),
                        xbv_sb[:, :].rearrange("p (h e) -> p h e", e=XD).unsqueeze(1).broadcast_to([P, NB, XH, XD]),
                        ALU.add).then_inc(s_vpad, 1)

                def decay(u):
                    dve.wait_ge(s_scA, 4 * a + u + 1)
                    if later(a):
                        dve.wait_ge(s_ret, a)
                    bk, cc = u // C, u % C
                    nc.vector.tensor_tensor(scD[:, bk, cc, :, :], SC_BANK[u][:, :].rearrange("p (j n) -> p j n", j=RJ),
                                            decay_sb[:, RJ * cc:RJ * (cc + 1), :], ALU.mult).then_inc(s_scD, 1)

                def split_hidden(u):
                    part = slice(2 * u, 2 * (u + 1))
                    dve.wait_ge(s_hT, UP * c + u + 1)
                    if u == 0:
                        if later(c):
                            dve.wait_ge(s_yC, c)
                    nc.vector.tensor_scalar(h_hi[:, part, :], h_in[:, u % 2, :, :], 1.0, None, ALU.mult)\
                        .then_inc(s_hhi, 1)
                    dve.wait_ge(s_hhi, UP * c + u + 1)
                    nc.vector.tensor_tensor(h_lo[:, part, :], h_in[:, u % 2, :, :],
                                            h_hi[:, part, :].bitcast(F32), ALU.subtract).then_inc(s_hlo, 1)

                def maxima(u):
                    dve.wait_ge(s_S, 8 * b + u + 1)
                    if u >= 2 or later(b):
                        dve.wait_ge(s_prob, 8 * b + u - 1)
                    nc.vector.tensor_reduce(negmax[:, u % 2, :], S_BANK[u][:, :].rearrange("p (g m) -> p g m", g=G),
                                            AX_X, ALU.min).then_inc(s_max, 1)

                def probT_odd(u):
                    dve.wait_ge(s_T, 8 * b + u + 1)
                    if u >= 2 or later(b):
                        dve.wait_ge(s_pv, 8 * b + u - 1)
                    nc.vector.tensor_copy(probT[:, u % 2, :, :],
                                          b1k[:, :].rearrange("p (g n) -> p g n", g=G)).then_inc(s_pTd, 1)

                def divide(seq):
                    dve.wait_ge(s_K, 2 * b + seq + 1)
                    if later(b):
                        dve.wait_ge(s_aT, b)
                    kv = c0[:, :].rearrange("p (h e) -> p h e", e=VP)
                    nc.vector.reciprocal(rden[:, seq, :], kv[:, :, XD]).then_inc(s_rden, 1)
                    dve.wait_ge(s_rden, 2 * b + seq + 1)
                    nc.vector.tensor_tensor(att[:, seq, :, :], kv[:, :, 0:XD],
                                            rden[:, seq, :].unsqueeze(2).broadcast_to([P, XH, XD]), ALU.mult)\
                        .then_inc(s_att, 1)

                if do_a:
                    decay(0)
                    decay(1)
                if do_c:
                    split_hidden(0)
                    split_hidden(1)
                if do_a:
                    decay(2)
                    decay(3)
                if do_b:
                    maxima(0)
                    maxima(1)
                if do_c:
                    split_hidden(2)
                    split_hidden(3)
                if do_b:
                    maxima(2)
                    maxima(3)
                    probT_odd(1)
                if do_a:
                    dve.wait_ge(s_sqA, a + 1)
                    nc.vector.tensor_reduce(varA[:, :], sqA[:, :, :], AX_X, ALU.add).then_inc(s_varA, 1)
                    dve.wait_ge(s_varA, 2 * a + 1)
                    nc.vector.tensor_scalar(varA[:, :], varA[:, :], 1.0 / RD, EPS, ALU.mult, ALU.add)\
                        .then_inc(s_varA, 1)
                if do_b:
                    maxima(4)
                    maxima(5)
                    probT_odd(3)
                    maxima(6)
                if do_a:
                    dve.wait_ge(s_rstA, a + 1)
                    if later(a):
                        dve.wait_ge(s_rnT, a)
                    nc.vector.tensor_tensor(rnA[:, :, :], a1[:, :].rearrange("p (h e) -> p h e", e=RD),
                                            rstA[:, :].unsqueeze(2).broadcast_to([P, NB * RH, RD]), ALU.mult)\
                        .then_inc(s_rnA, 1)
                if nextA:
                    dve.wait_ge(s_x, 16 * (a + 2))
                    statistics(a + 1, x_in, statA, mvA, s_lnA)
                if do_b:
                    maxima(7)
                if do_a:
                    dve.wait_ge(s_rnT, a + 1)
                    dve.wait_ge(s_sgA, 2 * (a + 1))
                    if later(a):
                        dve.wait_ge(s_yA, a)
                    for k in range(C):
                        nc.vector.scalar_tensor_tensor(out=outT[:, k, :], in0=a0[:, k * T:(k + 1) * T],
                                                       scalar=gn_sb[:, 0, k:k + 1], in1=sgA[:, k, :],
                                                       op0=ALU.mult, op1=ALU.add).then_inc(s_outT, 1)
                if do_b:
                    probT_odd(5)
                if nextA:
                    normalise(a + 1, x_in, mvA, rsA, xnA, s_rsA, s_xnA, s_TA)
                if do_a:
                    dve.wait_ge(s_yA, a + 1)
                    dve.wait_ge(s_keep, a + 1)
                    if do_b:
                        dve.wait_ge(s_x1b, b + 1)
                    nc.vector.tensor_tensor(x1[:, :, :], a1[:, :].rearrange("p (b d) -> p b d", b=NB),
                                            x_keep[:, :, :], ALU.add).then_inc(s_x1, 1)
                if do_b:
                    divide(0)
                if do_a:
                    dve.wait_ge(s_x1, a + 1)
                    statistics(a, x1, statB, mvB, s_lnB)
                if do_b:
                    probT_odd(7)
                if do_a:
                    normalise(a, x1, mvB, rsB, xnB, s_rsB, s_xnB, s_TxB)
                if do_b:
                    divide(1)
                if do_c:
                    dve.wait_ge(s_yC, c + 1)
                    dve.wait_ge(s_x2b, c + 1)
                    if later(c):
                        dve.wait_ge(s_out, 16 * c)
                    nc.vector.tensor_tensor(y_out[:, :, :], c1[:, :].rearrange("p (b d) -> p b d", b=NB),
                                            x2b[:, :, :], ALU.add).then_inc(s_yout, 1)
                if do_a:
                    dve.wait_ge(s_kTB, 2 * (a + 1))
                    if later(a):
                        dve.wait_ge(s_k0, ONE * a)
                    if later(a):
                        dve.wait_ge(s_k1, ONE * a)
                    if later(a):
                        dve.wait_ge(s_k23, TWO * a)
                    for h in range(2):
                        nc.vector.tensor_scalar(k_hi[:, h, :, :], kTB[:, :, :], head_of[:, h:h + 1], None, ALU.mult)\
                            .then_inc(s_khi, 1)
                if do_b:
                    dve.wait_ge(s_yB, b + 1)
                    dve.wait_ge(s_x1b, b + 1)
                    if do_c:
                        dve.wait_ge(s_x2b, c + 1)
                    nc.vector.tensor_tensor(x2[:, :, :], b0[:, :].rearrange("p (b d) -> p b d", b=NB),
                                            x1b[:, :, :], ALU.add).then_inc(s_x2, 1)
            dve.wait_ge(s_x, 16)
            statistics(0, x_in, statA, mvA, s_lnA)
            normalise(0, x_in, mvA, rsA, xnA, s_rsA, s_xnA, s_TA)
            dve.wait_ge(s_wH, 16 * WH_LOADS)
            nc.vector.tensor_reduce(wv_mean[:, :], wv_c[:, :, :], AX_X, ALU.add).then_inc(s_cent, 1)
            dve.wait_ge(s_cent, 1)
            nc.vector.tensor_scalar(wv_mean[:, :], wv_mean[:, :], 1.0 / RD, None, ALU.mult).then_inc(s_cent, 1)
            dve.wait_ge(s_cent, 2)
            nc.vector.tensor_tensor(wv_c[:, :, :], wv_c[:, :, :], wv_mean[:, :].unsqueeze(2).broadcast_to([P, C, RD]),
                                    ALU.subtract).then_inc(s_cent, 1)
            for w in (wq_bd, wk_bd, wv_bd):
                nc.vector.memset(w[:, :, :], 0.0).then_inc(s_cent, 1)
            dve.wait_ge(s_cent, 6)
            for w, src in ((wq_bd, wq_c), (wk_bd, wk_c), (wv_bd, wv_c)):
                for j in range(RJ):
                    rows = slice(RD * j, RD * (j + 1))
                    nc.vector.tensor_copy(w[rows, :, rows], src[rows, :, :]).then_inc(s_bd, 1)
            dve.wait_ge(s_wA, 16 * WA_LOADS)
            nc.vector.tensor_scalar(nbq[:, :], xb_sb[:, 0, :], -XSCALE, None, ALU.mult).then_inc(s_nbq, 1)
            dve.wait_ge(s_const, 9)
            nc.vector.tensor_reduce(head_of[:, :], ident[:, :].rearrange("p (r h k) -> p h r k", r=PR, h=2),
                                    AX_XY, ALU.add).then_inc(s_head, 1)
            dve.wait_ge(s_setT, 1)
            nc.vector.tensor_copy(wqT_bd[:, :, :], b0[:, 0:D].rearrange("p (c n) -> p c n", c=C))
            nc.vector.tensor_copy(wkT_bd[:, :, :], b0[:, D:2 * D].rearrange("p (c n) -> p c n", c=C))\
                .then_inc(s_setC, 1)
            dve.wait_ge(s_qk, 1)
            nc.vector.tensor_copy(qk_bd[:, :, :], b2k[:, 0:D].rearrange("p (c n) -> p c n", c=C))\
                .then_inc(s_setC, 1)
            dve.wait_ge(s_b1T, 1)
            nc.vector.tensor_copy(b1T[:, :], c0[:, 0:STEPS * FC]).then_inc(s_setC, 1)
            nc.vector.memset(q_bd[:, :, :], 0.0).then_inc(s_zerod, 1)
            dve.wait_ge(s_zerod, 1)
            dve.wait_ge(s_setC, 3)
            dve.wait_ge(s_head, 1)
            dve.wait_ge(s_nbq, 1)
            pipeline(dve, body)

        @block.tensor
        def _(pe):
            def mm(out, lhsT, rhs, start=True, stop=True):
                return nc.tensor.matmul(out, lhsT, rhs, start=start, stop=stop)

            def mm_split(out, lhsT, rhs, start=True, stop=True):
                mm(out, lhsT[0], rhs[0], start=start, stop=False)
                mm(out, lhsT[0], rhs[1], start=False, stop=False)
                return mm(out, lhsT[1], rhs[0], start=False, stop=stop)

            def transposes(out, src, done):
                for k in range(C):
                    for b in range(NB):
                        col = k * T + b * P
                        ins = nc.tensor.transpose(out[:, col:col + P], src[:, b, k * P:(k + 1) * P], ident[:, :])
                ins.then_inc(done, 1)

            def to_channels(out, w, xT, done):
                for m in range(C):
                    for k in range(C):
                        ins = mm(out[:, m * T:(m + 1) * T], w[:, k, m * P:(m + 1) * P], xT[:, k, :],
                                 start=(k == 0), stop=(k == C - 1))
                ins.then_inc(done, 1)

            def to_tokens(out, xT, w, done):
                for b in range(NB):
                    for k in range(C):
                        ins = mm(out[:, b * D:(b + 1) * D], xT[:, k, b * P:(b + 1) * P], w[:, k, :],
                                 start=(k == 0), stop=(k == C - 1))
                ins.then_inc(done, 1)

            def body(i, do_a, do_b, do_c, nextA):
                a, b, c = i, i - 1, i - 2

                def ret_scores(u):
                    bk, cc = u // C, u % C
                    if u == 0:
                        pe.wait_ge(s_silA, a + 1)
                    elif u == 1:
                        pe.wait_ge(s_vA, a + 1)
                    else:
                        if u >= 2 or later(a):
                            pe.wait_ge(s_scD, 4 * a + u - 1)
                    tok = slice(bk * P, (bk + 1) * P)
                    qv = q_bd[:, :, :].rearrange("p j (c b n) -> p j c b n", c=C, b=NB)
                    mm(SC_BANK[u][:, :].rearrange("p (j n) -> p j n", j=RJ), xTA[:, cc, tok], qv[:, :, cc, bk, :])\
                        .then_inc(s_scA, 1)

                def scores(u):
                    bk, g = u // 4, GROUP[u % 4]
                    cc, hh = g // 2, g % 2
                    if u == 0:
                        pe.wait_ge(s_q01, TWO * (b + 1))
                        pe.wait_ge(s_k0, ONE * (b + 1))
                        pe.wait_ge(s_k1, ONE * (b + 1))
                    if u == 2:
                        pe.wait_ge(s_q23, TWO * (b + 1))
                        pe.wait_ge(s_k23, TWO * (b + 1))
                    mm(S_BANK[u][:, :], ident_bf[:, :], mask_bf[:, :, :].rearrange("p g m -> p (g m)"),
                       start=True, stop=False)
                    tok = slice(bk * P, (bk + 1) * P)
                    for pair in range(2):
                        r = 2 * hh + pair
                        ins = mm(S_BANK[u][:, pair * 2 * P:(pair + 1) * 2 * P].rearrange("p (h m) -> p h m", h=2),
                                 q_st[:, r, cc, tok], k_st[:, r, :, cc, tok], start=False, stop=(pair == 1))
                    ins.then_inc(s_S, 1)

                def prob_transposes(u):
                    pe.wait_ge(s_prob, 8 * b + u + 1)
                    if u == 0:
                        pe.wait_ge(s_vpad, b + 1)
                    elif u % 2:
                        pe.wait_ge(s_pTa, 4 * b + u // 2 + 1)
                    else:
                        pe.wait_ge(s_pTd, 4 * b + u // 2)
                    for g in range(G):
                        ins = nc.tensor.transpose(b1k[:, g * P:(g + 1) * P], prob[:, u % 2, g, :], ident[:, :])
                    ins.then_inc(s_T, 1)

                def with_values(u):
                    bk, g = u // 4, GROUP[u % 4]
                    if u % 2:
                        pe.wait_ge(s_pTd, 4 * b + u // 2 + 1)
                    else:
                        pe.wait_ge(s_pTa, 4 * b + u // 2 + 1)
                    if u == 0:
                        pe.wait_ge(s_vpad, b + 1)
                        if later(b):
                            pe.wait_ge(s_pvT, 2 * b)
                    if u == 4:
                        pe.wait_ge(s_pvT, 2 * b + 1)
                    for h in range(G):
                        ins = mm(b3[VP * h:VP * (h + 1), g * P:(g + 1) * P], v_pad[:, bk, G * g + h, :],
                                 probT[:, u % 2, h, :])
                    ins.then_inc(s_pv, 1)

                def values_to_tokens(seq):
                    pe.wait_ge(s_pvT, 2 * b + seq + 1)
                    for g in range(4):
                        ins = nc.tensor.transpose(c0[:, g * P:(g + 1) * P], pvT[:, seq, g * P:(g + 1) * P],
                                                  ident[:, :])
                    ins.then_inc(s_K, 1)

                def up(u, bank):
                    pe.wait_ge(s_w1lo, UP * c + u + 1)
                    for k2 in range(2):
                        f = 2 * u + k2
                        for k in range(C):
                            ins = mm_split(bank[:, k2 * T:(k2 + 1) * T],
                                           [w[:, k, f * P:(f + 1) * P] for w in (w1_hi, w1_lo)],
                                           [t[:, k, :] for t in (xTC_hi, xTC_lo)], start=(k == 0), stop=(k == C - 1))
                    ins.then_inc(s_up, 1)

                def down(piece):
                    bk, quarter = piece // UP, piece % UP
                    if bk == 0:
                        pe.wait_ge(s_hlo, UP * c + quarter + 1)
                        pe.wait_ge(s_w2lo, UP * c + quarter + 1)
                    for f in (2 * quarter, 2 * quarter + 1):
                        ins = mm_split(c1[:, bk * D:(bk + 1) * D],
                                       [h[:, f, bk * P:(bk + 1) * P] for h in (h_hi, h_lo)],
                                       [w[:, f, :] for w in (w2_hi, w2_lo)], start=(f == 0), stop=(f == FC - 1))
                    if piece == NB * UP - 1:
                        ins.then_inc(s_yC, 1)

                if do_a:
                    if later(a):
                        pe.wait_ge(s_kTB, 2 * a)
                    for k in range(C):
                        ins = mm(a1[:, k * T:(k + 1) * T], qk_bd[:, k, :], xTA[:, k, :])
                    ins.then_inc(s_qA, 1)
                if do_b:
                    pe.wait_ge(s_xnB, 2 * (b + 1))
                    if later(b):
                        pe.wait_ge(s_x2, b)
                    transposes(b0, xnB, s_TxB)
                    to_tokens(b1k, cTB, xWv_sb, s_vB)
                if do_a:
                    pe.wait_ge(s_qbda, 2 * (a + 1))
                    pe.wait_ge(s_qbdd, 2 * (a + 1))
                    for bk in range(NB):
                        for k in range(C):
                            col = bk * D + k * P
                            ins = mm(a1[:, col:col + P], xTA[:, k, bk * P:(bk + 1) * P], wv_bd[:, k, :])
                    ins.then_inc(s_vAp, 1)
                if do_c:
                    pe.wait_ge(s_xnC, 2 * (c + 1))
                    pe.wait_ge(s_att, 2 * (c + 1))
                    transposes(c0, xnC, s_TC)
                if do_b:
                    pe.wait_ge(s_xTB, b + 1)
                    to_channels(b0, xWq_sb, xTB, s_qB)
                if do_c:
                    pe.wait_ge(s_xTClo, c + 1)
                    if later(c):
                        pe.wait_ge(s_yout, c)
                    up(0, c1)
                    up(1, c0)
                if do_a:
                    ret_scores(0)
                    ret_scores(1)
                if do_c:
                    pe.wait_ge(s_hT, UP * c + 1)
                    up(2, c1)
                    pe.wait_ge(s_hT, UP * c + 2)
                    up(3, c0)
                if do_a:
                    ret_scores(2)
                    ret_scores(3)
                if do_b:
                    scores(0)
                    scores(1)
                if do_c:
                    pe.wait_ge(s_hT, UP * (c + 1))
                if do_b:
                    scores(2)
                if do_a:
                    pe.wait_ge(s_scD, 4 * (a + 1))
                    for cc in range(C):
                        for bk in range(NB):
                            for j in range(RJ):
                                h = RJ * cc + j
                                ins = mm(a0[RD * j:RD * (j + 1), cc * T + bk * P:cc * T + (bk + 1) * P],
                                         vA[:, bk, RD * h:RD * (h + 1)], scD[:, bk, cc, j, :])
                    ins.then_inc(s_ret, 1)
                if do_c:
                    down(0)
                    down(1)
                if do_b:
                    prob_transposes(0)
                    scores(3)
                if do_a:
                    pe.wait_ge(s_retT, a + 1)
                    for bk in range(NB):
                        for cc in range(C):
                            col = bk * D + cc * P
                            ins = nc.tensor.transpose(a1[:, col:col + P], retT[:, cc, bk, :], ident[:, :])
                    ins.then_inc(s_rtok, 1)
                if do_b:
                    prob_transposes(1)
                    scores(4)
                    with_values(0)
                if do_c:
                    down(2)
                if do_b:
                    prob_transposes(2)
                    scores(5)
                    with_values(1)
                if do_c:
                    down(3)
                if do_b:
                    prob_transposes(3)
                    scores(6)
                    with_values(2)
                if do_c:
                    down(4)
                if do_b:
                    with_values(3)
                    prob_transposes(4)
                    scores(7)
                if do_c:
                    down(5)
                if do_b:
                    prob_transposes(5)
                    values_to_tokens(0)
                if do_a:
                    pe.wait_ge(s_rnA, a + 1)
                    for k in range(C):
                        for bk in range(NB):
                            col = k * T + bk * P
                            src = rnA[:, :, :].rearrange("p (b h) e -> p b (h e)", b=NB)
                            ins = nc.tensor.transpose(a0[:, col:col + P], src[:, bk, k * P:(k + 1) * P], ident[:, :])
                    ins.then_inc(s_rnT, 1)
                if do_b:
                    with_values(4)
                if do_c:
                    down(6)
                if do_a:
                    pe.wait_ge(s_outT, 2 * (a + 1))
                    to_tokens(a1, outT, W2_sb, s_yA)
                if do_b:
                    prob_transposes(6)
                    with_values(5)
                if nextA:
                    transposed_x(a + 1)
                if do_b:
                    prob_transposes(7)
                    with_values(6)
                if do_c:
                    down(7)
                if do_b:
                    with_values(7)
                if do_a:
                    pe.wait_ge(s_c, 16 * (a + 1))
                    if do_b:
                        pe.wait_ge(s_pTd, 4 * (b + 1))
                    transposes(b1k, c_in, s_TcB)
                if nextA:
                    gate(a + 1, 0)
                if do_b:
                    pe.wait_ge(s_att, 2 * b + 1)
                    values_to_tokens(1)
                if nextA:
                    gate(a + 1, 1)
                    gate(a + 1, 2)
                if do_b:
                    pe.wait_ge(s_att, 2 * (b + 1))
                    attv = att[:, :, :, :].rearrange("p b h e -> p b (h e)")
                    transposes(b2k, attv, s_aT)
                if do_a:
                    pe.wait_ge(s_cTB, a + 1)
                    pe.wait_ge(s_x1, a + 1)
                    to_channels(a1, xWk_sb, cTB, s_kB)
                if do_b:
                    pe.wait_ge(s_attT, b + 1)
                    to_tokens(b0, attT, xWo_sb, s_yB)
                if nextA:
                    gate(a + 1, 3)

            def transposed_x(step):
                pe.wait_ge(s_xnA, 2 * (step + 1))
                if later(step):
                    pe.wait_ge(s_outT, 2 * step)
                transposes(a0, xnA, s_TA)

            def gate(step, piece):
                m, k = piece // C, piece % C
                if piece == 0:
                    pe.wait_ge(s_xTA, step + 1)
                ins = mm(a0[:, m * T:(m + 1) * T], W1_sb[:, k, m * P:(m + 1) * P], xTA[:, k, :],
                         start=(k == 0), stop=(k == C - 1))
                if piece == C * C - 1:
                    ins.then_inc(s_gA, 1)

            pe.wait_ge(s_const, 9)
            transposed_x(0)
            pe.wait_ge(s_wA, 16 * WA_LOADS)
            for n in range(4):
                gate(0, n)
            pe.wait_ge(s_bd, 3 * RJ)
            for n, w in enumerate((wq_bd, wk_bd)):
                for k in range(C):
                    ins = nc.tensor.transpose(b0[:, (C * n + k) * P:(C * n + k + 1) * P], w[:, k, :], ident[:, :])
            ins.then_inc(s_setT, 1)
            pe.wait_ge(s_setC, 1)
            for k in range(C):
                ins = mm(b2k[:, k * P:(k + 1) * P], wqT_bd[:, k, :], wkT_bd[:, k, :])
            ins.then_inc(s_qk, 1)
            pe.wait_ge(s_wB, 16 * WB_LOADS)
            pe.wait_ge(s_xWq, 1)
            n = STEPS * FC
            nc.tensor.transpose(c0[:, 0:n], b1_rows[:, :], ident[0:n, 0:n]).then_inc(s_b1T, 1)
            pe.wait_ge(s_setC, 3)
            pipeline(pe, body)


_INS = ['x', 'ctx_1024', 'L0_attn_Wq', 'L0_attn_Wk', 'L0_attn_Wv', 'L0_attn_W1', 'L0_attn_W2', 'L0_attn_gn_w',
        'L0_attn_gn_b', 'L0_xattn_Wq', 'L0_xattn_bq', 'L0_xattn_Wk', 'L0_xattn_bk', 'L0_xattn_Wv', 'L0_xattn_bv',
        'L0_xattn_Wo', 'L0_xattn_bo', 'L0_ffn_w1', 'L0_ffn_b1', 'L0_ffn_w2', 'L0_ffn_b2']


def kernel(**inputs):
    import concourse.bacc as bacc
    from concourse.bass_utils import run_bass_kernel_spmd

    nc = bacc.Bacc("TRN2", target_bir_lowering=False, num_devices=1)
    arrays, args = {}, []
    for name in _INS:
        arrays[f"in_{name}"] = np.ascontiguousarray(inputs[name])
    arrays["in_decay"] = decay_table()
    for name, a in arrays.items():
        args.append(nc.dram_tensor(name, a.shape, mybir.dt.from_np(a.dtype), kind="ExternalInput").ap())
    out = nc.dram_tensor("out", (STEPS * NB, P, D), F32, kind="ExternalOutput").ap()
    decoder_kernel(nc, *args, out)
    r = run_bass_kernel_spmd(nc, [arrays], core_ids=[0])
    return r.results[0]["out"]
```

```python
from contextlib import ExitStack

import numpy as np

import concourse.bass as bass
from concourse import mybir
from concourse.alu_op_type import AluOpType as ALU

ACT = mybir.ActivationFunctionType
F32 = mybir.dt.float32
F32R = mybir.dt.float32r
BF16 = mybir.dt.bfloat16
AX_X = mybir.AxisListType.X
AX_XY = mybir.AxisListType.XY

P = 128
D = 256
C = D // P
NB = 2
T = NB * P
STEPS = 8
RH, RD = 8, 32
XH, XD = 16, 16
RJ = P // RD
PR = P // (2 * XD)
QJ = RJ - 1
G = 4
VP = 32
FF = 1024
FC = FF // P
UP = FC // 2
EPS = 1e-5
MASKED = 1e30
XSCALE = float(XD) ** -0.5
ONE = 3 * 16
TWO = 2 * ONE
WH_LOADS = 3
WA_LOADS = 7
WB_LOADS = 7


def decay_table():
    lin = np.linspace(np.log(1.0 / 512.0), np.log(1.0 / 32.0), RH)
    gammas = (1.0 - np.exp(lin)).astype(np.float32)
    diff = np.arange(P)[None, :] - np.arange(P)[:, None]
    powers = gammas.astype(np.float64)[None, :, None] ** np.maximum(diff, 0)[:, None, :]
    return np.where(diff[:, None, :] >= 0, powers, 0.0).astype(np.float32)


def decoder_kernel(nc, x, ctx_in, Wq, Wk, Wv, W1, W2, gn_w, gn_b, xWq, xbq, xWk, xbk, xWv, xbv, xWo, xbo,
                   w1, b1, w2, b2, decay, out):
    ctx = ExitStack()
    with ctx:
        def sb(name, shape, dt=F32):
            return ctx.enter_context(nc.sbuf_tensor(name, shape, dt))

        def bank(name):
            return ctx.enter_context(nc.psum_tensor(name, [P, 512], F32))

        def signal(name):
            return ctx.enter_context(nc.semaphore(name))

        ident = sb("ident", [P, P])
        ident_bf = sb("ident_bf", [P, P], BF16)
        mask_bf = sb("mask_bf", [P, G, P], BF16)
        decay_sb = sb("decay_sb", [P, RH, P])
        minus_half = sb("minus_half", [P, NB * RH])
        wq_c = sb("wq_c", [P, C, RD])
        wk_c = sb("wk_c", [P, C, RD])
        wv_c = sb("wv_c", [P, C, RD])
        wv_mean = sb("wv_mean", [P, C])
        wv_bd = sb("wv_bd", [P, C, P])
        qk_bd = sb("qk_bd", [P, C, P])
        W1_sb = sb("W1_sb", [P, C, D])
        W2_sb = sb("W2_sb", [P, C, D])
        gn_sb = sb("gn_sb", [P, 2, C])
        xWq_hi = sb("xWq_hi", [P, C, D], F32R)
        xWq_lo = sb("xWq_lo", [P, C, D], F32R)
        xWk_hi = sb("xWk_hi", [P, C, D], F32R)
        xWk_lo = sb("xWk_lo", [P, C, D], F32R)
        xWv_hi = sb("xWv_hi", [P, C, D], F32R)
        xWv_lo = sb("xWv_lo", [P, C, D], F32R)
        xWo_hi = sb("xWo_hi", [P, C, D], F32R)
        xWo_lo = sb("xWo_lo", [P, C, D], F32R)
        xb_sb = sb("xb_sb", [P, 2, C])
        nbq = sb("nbq", [P, C])
        spare = sb("spare", [P, 1])
        head_of = sb("head_of", [P, 2])
        xbv_sb = sb("xbv_sb", [P, D])
        xbo_sb = sb("xbo_sb", [P, D])
        b1_rows = sb("b1_rows", [STEPS * FC, P])
        b1T = sb("b1T", [P, STEPS * FC])

        x_in = sb("x_in", [P, NB, D])
        x_keep = sb("x_keep", [P, NB, D])
        statA = sb("statA", [P, NB, 6])
        mvA = sb("mvA", [P, NB, 2])
        rsA = sb("rsA", [P, NB])
        xnA = sb("xnA", [P, NB, D])
        xTA = sb("xTA", [P, C, T])
        q_bd = sb("q_bd", [P, RJ, C * T])
        thA = sb("thA", [P, C, T])
        silA = sb("silA", [P, C, T])
        vA = sb("vA", [P, NB, D])
        scD = sb("scD", [P, NB, C, RJ, P])
        retT = sb("retT", [P, C, NB, P])
        sqA = thA[:, :, :].rearrange("p c t -> p (c t)").rearrange("p (h e) -> p h e", e=RD)
        varA = sb("varA", [P, NB * RH])
        rstA = sb("rstA", [P, NB * RH])
        rnA = retT[:, :, :, :].rearrange("p c b n -> p (c b n)").rearrange("p (h e) -> p h e", e=RD)
        outT = sb("outT", [P, C, T])
        x1 = sb("x1", [P, NB, D])

        c_in = sb("c_in", [P, NB, D])
        x1b = sb("x1b", [P, NB, D])
        statB = sb("statB", [P, NB, 6])
        mvB = sb("mvB", [P, NB, 2])
        rsB = sb("rsB", [P, NB])
        xnB = sb("xnB", [P, NB, D])
        xTB_hi = sb("xTB_hi", [P, C, T], F32R)
        xTB_lo = sb("xTB_lo", [P, C, T], F32R)
        cTB_hi = sb("cTB_hi", [P, C, T], F32R)
        cTB_lo = sb("cTB_lo", [P, C, T], F32R)
        q_hi = sb("q_hi", [P, C, T], F32R)
        q_lo = sb("q_lo", [P, C, T], F32R)
        kTB = retT[:, :, :, :].rearrange("p c b n -> p c (b n)")
        k_hi = sb("k_hi", [P, 2, C, T], F32R)
        k_lo = sb("k_lo", [P, 2, C, T], F32R)
        q_st = sb("q_st", [P, PR, C, T], F32R)
        k_st = sb("k_st", [P, PR, 2, C, T], F32R)
        v_pad = sb("v_pad", [P, NB, XH, VP])
        negmax = sb("negmax", [P, 2, G])
        prob = sb("prob", [P, 2, G, P])
        probT = sb("probT", [P, 2, G, P])
        pvT = sb("pvT", [P, 512])
        rden = sb("rden", [P, NB, XH])
        att = sb("att", [P, NB, XH, XD])
        attT_hi = sb("attT_hi", [P, C, T], F32R)
        attT_lo = sb("attT_lo", [P, C, T], F32R)
        x2 = sb("x2", [P, NB, D])

        x2b = sb("x2b", [P, NB, D])
        statC = sb("statC", [P, NB, 6])
        mvC = sb("mvC", [P, NB, 2])
        rsC = sb("rsC", [P, NB])
        xnC = sb("xnC", [P, NB, D])
        xTC_hi = sb("xTC_hi", [P, C, T], F32R)
        xTC_lo = sb("xTC_lo", [P, C, T], F32R)
        w1_hi = sb("w1_hi", [P, C, FF], F32R)
        w1_lo = sb("w1_lo", [P, C, FF], F32R)
        w2_hi = sb("w2_hi", [P, FC, D], F32R)
        w2_lo = sb("w2_lo", [P, FC, D], F32R)
        w_in = sb("w_in", [P, C * FF])
        b1_cur = sb("b1_cur", [P, FC])
        b2_cur = sb("b2_cur", [P, D])
        h_hi = sb("h_hi", [P, FC, T], F32R)
        h_lo = sb("h_lo", [P, FC, T], F32R)
        h_in = probT[:, :, :, :].rearrange("p u g n -> p u (g n)").rearrange("p u (k t) -> p u k t", k=2)

        wq_bd, wk_bd, wqT_bd, wkT_bd = [scD[:, 0, n // 2, 2 * (n % 2):2 * (n % 2) + C, :] for n in range(4)]

        def keys_of(step):
            return prob[:, :, :, :].rearrange("p u g n -> p (u g n)")[:, 0:C * T].rearrange("p (c t) -> p c t", c=C) \
                if isinstance(step, int) and step == 0 else kTB

        w1_in = w_in[:, :].rearrange("p (c f) -> p c f", c=C)
        w2_in = w_in[:, :].rearrange("p (f d) -> p f d", f=FC)
        xw_in = w_in[:, :].rearrange("p (w c d) -> p w c d", w=4, c=C)

        a0, a1, b0, b1k, b2k, b3, c0, c1 = [bank(n) for n in ("a0", "a1", "b0", "b1k", "b2k", "b3", "c0", "c1")]

        SC_BANK = [a0, a1, a0, a1]
        S_BANK = [b2k, b0, c0, b2k, b0, c0, b2k, b0]
        KEYS_BANK = {True: a1, False: b2k}
        GROUP = [0, 2, 1, 3]

        s_wH = signal("s_wH")
        s_wA = signal("s_wA")
        s_wB = signal("s_wB")
        s_nbq = signal("s_nbq")
        s_head = signal("s_head")
        s_xWhi = signal("s_xWhi")
        s_xWlo = signal("s_xWlo")
        s_b1T = signal("s_b1T")
        s_zero = signal("s_zero")
        s_zerod = signal("s_zerod")
        s_apart = {nc.vector.engine: ctx.enter_context(nc.semaphore("s_apart_dve")),
                   nc.gpsimd.engine: ctx.enter_context(nc.semaphore("s_apart_pool"))}
        s_const = signal("s_const")
        s_cent = signal("s_cent")
        s_bd = signal("s_bd")
        s_setT = signal("s_setT")
        s_setC = signal("s_setC")
        s_qk = signal("s_qk")
        s_x = signal("s_x")
        s_lnA = signal("s_lnA")
        s_rsA = signal("s_rsA")
        s_xnA = signal("s_xnA")
        s_keep = signal("s_keep")
        s_TA = signal("s_TA")
        s_xTA = signal("s_xTA")
        s_qA = signal("s_qA")
        s_qbda = signal("s_qbda")
        s_qbdd = signal("s_qbdd")
        s_gA = signal("s_gA")
        s_thA = signal("s_thA")
        s_silh = signal("s_silh")
        s_silA = signal("s_silA")
        s_sgA = signal("s_sgA")
        s_vAp = signal("s_vAp")
        s_vA = signal("s_vA")
        s_scA = signal("s_scA")
        s_scD = signal("s_scD")
        s_ret = signal("s_ret")
        s_retT = signal("s_retT")
        s_rtok = signal("s_rtok")
        s_sqA = signal("s_sqA")
        s_varA = signal("s_varA")
        s_rstA = signal("s_rstA")
        s_rnA = signal("s_rnA")
        s_rnT = signal("s_rnT")
        s_outT = signal("s_outT")
        s_yA = signal("s_yA")
        s_x1 = signal("s_x1")

        s_c = signal("s_c")
        s_lnB = signal("s_lnB")
        s_rsB = signal("s_rsB")
        s_xnB = signal("s_xnB")
        s_x1b = signal("s_x1b")
        s_TxB = signal("s_TxB")
        s_TcB = signal("s_TcB")
        s_xTB = signal("s_xTB")
        s_xTBlo = signal("s_xTBlo")
        s_cTB = signal("s_cTB")
        s_cTBlo = signal("s_cTBlo")
        s_qB = signal("s_qB")
        s_qhi = signal("s_qhi")
        s_qlo = signal("s_qlo")
        s_q01 = signal("s_q01")
        s_q23 = signal("s_q23")
        s_kB = signal("s_kB")
        s_kTB = signal("s_kTB")
        s_khi = signal("s_khi")
        s_klo = signal("s_klo")
        s_k0 = signal("s_k0")
        s_k1 = signal("s_k1")
        s_k23 = signal("s_k23")
        s_vB = signal("s_vB")
        s_vpad = signal("s_vpad")
        s_S = signal("s_S")
        s_max = signal("s_max")
        s_prob = signal("s_prob")
        s_T = signal("s_T")
        s_pTa = signal("s_pTa")
        s_pTd = signal("s_pTd")
        s_pv = signal("s_pv")
        s_pvT = signal("s_pvT")
        s_K = signal("s_K")
        s_rden = signal("s_rden")
        s_att = signal("s_att")
        s_aT = signal("s_aT")
        s_attT = signal("s_attT")
        s_attTlo = signal("s_attTlo")
        s_yB = signal("s_yB")
        s_x2 = signal("s_x2")

        s_w1 = signal("s_w1")
        s_w2 = signal("s_w2")
        s_b2 = signal("s_b2")
        s_b1c = signal("s_b1c")
        s_lnC = signal("s_lnC")
        s_rsC = signal("s_rsC")
        s_xnC = signal("s_xnC")
        s_x2b = signal("s_x2b")
        s_TC = signal("s_TC")
        s_xTC = signal("s_xTC")
        s_xTClo = signal("s_xTClo")
        s_w1hi = signal("s_w1hi")
        s_w1lo = signal("s_w1lo")
        s_w2hi = signal("s_w2hi")
        s_w2lo = signal("s_w2lo")
        s_up = signal("s_up")
        s_hT = signal("s_hT")
        s_hhi = signal("s_hhi")
        s_hlo = signal("s_hlo")
        s_yC = signal("s_yC")
        s_yout = signal("s_yout")
        s_y_half = signal("s_y_half")
        s_yout_half = signal("s_yout_half")
        s_out = signal("s_out")

        x_v = x.rearrange("(s b) n d -> s n b d", b=NB)
        c_v = ctx_in.rearrange("(s b) n d -> s n b d", b=NB)
        out_v = out.rearrange("(s b) n d -> s n b d", b=NB)
        w1_v = w1.rearrange("e (c p) f -> e p c f", p=P)
        w2_v = w2.rearrange("e (c p) d -> e p c d", p=P)
        b1_v = b1.rearrange("e (f p) -> (e f) p", p=P)

        def chunked(w):
            return w.rearrange("(c p) n -> p c n", p=P)

        def heads(w):
            return w.rearrange("(c j) d e -> (j d) c e", c=C)

        def later(step):
            return not isinstance(step, int) or step > 0

        def wait_apart(eng):
            eng.sem_inc(s_apart[eng.engine], 1)

        def pipeline(eng, body):
            body(0, True, False, False, True)
            body(1, True, True, False, True)
            body(2, True, True, True, True)
            with eng.Fori(3, STEPS - 1) as i:
                body(i, True, True, True, True)
            body(STEPS - 1, True, True, True, False)
            body(STEPS, False, True, True, False)
            body(STEPS + 1, False, False, True, False)

        def stack_k(eng, r, src, part, done):
            rows = slice(2 * XD * r, 2 * XD * (r + 1))
            to = slice(2 * XD * part, 2 * XD * (part + 1))
            eng.dma_start(k_st[to, r, :, :, :].bitcast(F32), src[rows, :, :, :].bitcast(F32)).then_inc(done, 16)

        block = ctx.enter_context(nc.Block())

        @block.sync
        def _(sp):
            sp.dma_start(x_in[:, :, :], x_v[0]).then_inc(s_x, 16)
            for dst, src in ((wq_c, Wq), (wk_c, Wk), (wv_c, Wv)):
                sp.dma_start(dst[:, :, :], heads(src)).then_inc(s_wH, 16)
            sp.dma_start(W1_sb[:, :, :], chunked(W1)).then_inc(s_wA, 16)
            sp.dma_start(decay_sb[:, :, :], decay).then_inc(s_wA, 16)
            sp.dma_start(W2_sb[:, :, :], chunked(W2)).then_inc(s_wA, 16)
            with nc.allow_non_contiguous_dma(reason="four short vectors, once"):
                for dst, src in ((gn_sb[:, 0, :], gn_w), (gn_sb[:, 1, :], gn_b),
                                 (xb_sb[:, 0, :], xbq), (xb_sb[:, 1, :], xbk)):
                    sp.dma_start(dst, src.rearrange("(c p) -> p c", p=P)).then_inc(s_wA, 16)
            sp.dma_start(c_in[:, :, :], c_v[0]).then_inc(s_c, 16)
            for n, src in enumerate((xWq, xWk, xWv, xWo)):
                sp.dma_start(xw_in[:, n, :, :], chunked(src)).then_inc(s_wB, 16)
            for dst, src in ((xbv_sb, xbv), (xbo_sb, xbo)):
                sp.dma_start(dst[:, :], src.partition_broadcast(P)).then_inc(s_wB, 16)
            sp.dma_start(b1_rows[:, :], b1_v).then_inc(s_wB, 16)
            sp.dma_start(b2_cur[:, :], b2[0].partition_broadcast(P)).then_inc(s_b2, 16)
            sp.wait_ge(s_zero, 2)

            def body(i, do_a, do_b, do_c, nextA):
                a, b, c = i, i - 1, i - 2
                if do_b:
                    sp.wait_ge(s_khi, 2 * (b + 1))
                    stack_k(sp, 0, k_hi, 0, s_k0)
                    stack_k(sp, 0, k_hi, 2, s_k0)
                    sp.wait_ge(s_klo, 2 * (b + 1))
                    stack_k(sp, 0, k_lo, 1, s_k0)
                if do_b:
                    sp.wait_ge(s_qhi, 2 * (b + 1))
                    for pairs, done in (((0, 1), s_q01), ((2, 3), s_q23)):
                        for part, src in enumerate((q_hi, q_hi, q_lo)):
                            if part == 2 and pairs == (0, 1):
                                sp.wait_ge(s_qlo, 2 * (b + 1))
                            for r in pairs:
                                rows = slice(2 * XD * r, 2 * XD * (r + 1))
                                to = slice(2 * XD * part, 2 * XD * (part + 1))
                                sp.dma_start(q_st[to, r, :, :].bitcast(F32), src[rows, :, :].bitcast(F32))\
                                    .then_inc(done, 16)
                if do_a and do_b:
                    sp.wait_ge(s_TcB, b + 1)
                    sp.dma_start(c_in[:, :, :], c_v[a]).then_inc(s_c, 16)
                if nextA:
                    sp.wait_ge(s_xnA, 2 * (a + 1))
                    sp.wait_ge(s_keep, a + 1)
                    sp.dma_start(x_in[:, :, :], x_v[a + 1]).then_inc(s_x, 16)
                if isinstance(i, int) and i == 0:
                    sp.wait_ge(s_xWlo, 4)
                    sp.dma_start(w1_in, w1_v[0]).then_inc(s_w1, 16)
                if do_b and do_c:
                    sp.wait_ge(s_w2lo, UP * (c + 1))
                    sp.dma_start(w1_in, w1_v[b]).then_inc(s_w1, 16)
                    sp.wait_ge(s_x2b, c + 1)
                    sp.dma_start(b2_cur[:, :], b2[b].partition_broadcast(P)).then_inc(s_b2, 16)
                if do_b:
                    sp.wait_ge(s_w1lo, UP * (b + 1))
                    sp.dma_start(w2_in, w2_v[b]).then_inc(s_w2, 16)
                if do_c and not do_b:
                    sp.wait_ge(s_yout_half, 1)
                    sp.dma_start(out_v[c][:, 0:1, :], x2b[:, 0:1, :]).then_inc(s_out, 16)
                    sp.wait_ge(s_yout, c + 1)
                    sp.dma_start(out_v[c][:, 1:2, :], x2b[:, 1:2, :]).then_inc(s_out, 16)
                elif do_c:
                    sp.wait_ge(s_yout, c + 1)
                    sp.dma_start(out_v[c], x2b[:, :, :]).then_inc(s_out, 16)

            pipeline(sp, body)
            sp.wait_ge(s_out, 16 * (STEPS + 1))

        @block.gpsimd
        def _(pool):
            pool.memset(ident[:, :], 0.0).then_inc(s_const, 1)
            pool.memset(ident_bf[:, :], 0.0).then_inc(s_const, 1)
            pool.memset(mask_bf[:, :, :], 0.0).then_inc(s_const, 1)
            pool.wait_ge(s_const, 3)
            for m in (ident, ident_bf):
                pool.affine_select(out=m[:, :], in_=m[:, :], compare_op=ALU.not_equal, fill=1.0, base=0,
                                   pattern=[[-1, P]], channel_multiplier=1).then_inc(s_const, 1)
            pool.affine_select(out=mask_bf[:, :, :], in_=mask_bf[:, :, :], compare_op=ALU.is_ge, fill=MASKED,
                               base=0, pattern=[[0, G], [-1, P]], channel_multiplier=1)\
                .then_inc(s_const, 1)
            pool.memset(minus_half[:, :], -0.5).then_inc(s_const, 1)
            pool.memset(v_pad[:, :, :, XD:XD + 1], 1.0).then_inc(s_const, 1)
            pool.memset(v_pad[:, :, :, XD + 1:VP], 0.0).then_inc(s_const, 1)
            pool.wait_ge(s_const, 9)

            def rsqrt(step, out, in_, s_in, per_step, s_out, n):
                pool.wait_ge(s_in, per_step * (step + 1))
                pool.tensor_tensor(out, in_, minus_half[:, 0:n], ALU.pow).then_inc(s_out, 1)

            def body(i, do_a, do_b, do_c, nextA):
                a, b, c = i, i - 1, i - 2
                if do_c:
                    rsqrt(c, rsC[:, :], mvC[:, :, 1], s_lnC, 4, s_rsC, NB)
                if do_b:
                    pool.wait_ge(s_khi, 2 * (b + 1))
                    wait_apart(pool)
                    for r, done in ((1, s_k1), (2, s_k23)):
                        stack_k(pool, r, k_hi, 0, done)
                        stack_k(pool, r, k_hi, 2, done)
                    pool.wait_ge(s_klo, 2 * (b + 1))
                    wait_apart(pool)
                    stack_k(pool, 1, k_lo, 1, s_k1)
                    stack_k(pool, 2, k_lo, 1, s_k23)
                    stack_k(pool, 3, k_hi, 0, s_k23)
                    stack_k(pool, 3, k_hi, 2, s_k23)
                    stack_k(pool, 3, k_lo, 1, s_k23)
                if do_c:
                    for u in range(UP):
                        part = slice(2 * u, 2 * (u + 1))
                        pool.wait_ge(s_w2hi, UP * c + u + 1)
                        pool.tensor_tensor(w2_lo[:, part, :], w2_in[:, part, :],
                                           w2_hi[:, part, :].bitcast(F32), ALU.subtract).then_inc(s_w2lo, 1)
                if do_a:
                    if later(a):
                        pool.wait_ge(s_x1, a)
                    wait_apart(pool)
                    pool.tensor_scalar(x_keep[:, :, :], x_in[:, :, :], 1.0, None, ALU.mult).then_inc(s_keep, 1)
                if do_a:
                    pool.wait_ge(s_silA, a + 1)
                    wait_apart(pool)
                    for k in range(C):
                        pool.tensor_scalar(silA[:, k, :], silA[:, k, :], 0.5, gn_sb[:, 1, k:k + 1],
                                           ALU.mult, ALU.add).then_inc(s_sgA, 1)
                if do_a:
                    rsqrt(a, rstA[:, :], varA[:, :], s_varA, 2, s_rstA, NB * RH)
                if do_b:
                    if isinstance(i, int) and i == 1:
                        pool.wait_ge(s_wB, 16 * WB_LOADS)
                    pool.wait_ge(s_x1, b + 1)
                    if later(b):
                        pool.wait_ge(s_x2, b)
                    pool.tensor_tensor(x1b[:, :, :], x1[:, :, :],
                                       xbo_sb[:, :].unsqueeze(1).broadcast_to([P, NB, D]), ALU.add)\
                        .then_inc(s_x1b, 1)
                if do_b:
                    for u in range(UP):
                        part = slice(2 * P * u, 2 * P * (u + 1))
                        if u == 1 and nextA:
                            rsqrt(a + 1, rsA[:, :], mvA[:, :, 1], s_lnA, 4, s_rsA, NB)
                        pool.wait_ge(s_w1hi, UP * b + u + 1)
                        pool.tensor_tensor(w1_lo[:, :, part], w1_in[:, :, part],
                                           w1_hi[:, :, part].bitcast(F32), ALU.subtract).then_inc(s_w1lo, 1)
                elif nextA:
                    rsqrt(a + 1, rsA[:, :], mvA[:, :, 1], s_lnA, 4, s_rsA, NB)
                if do_c:
                    pool.wait_ge(s_b2, 16 * (c + 1))
                    pool.wait_ge(s_x2, c + 1)
                    if later(c):
                        pool.wait_ge(s_out, 16 * c)
                    pool.tensor_tensor(x2b[:, :, :], x2[:, :, :],
                                       b2_cur[:, :].unsqueeze(1).broadcast_to([P, NB, D]), ALU.add)\
                        .then_inc(s_x2b, 1)
                if do_a:
                    rsqrt(a, rsB[:, :], mvB[:, :, 1], s_lnB, 4, s_rsB, NB)

            rsqrt(0, rsA[:, :], mvA[:, :, 1], s_lnA, 4, s_rsA, NB)
            pool.memset(q_st[:, :, :, :].bitcast(F32), 0.0).then_inc(s_zero, 1)
            pool.memset(k_st[:, :, :, :, :].bitcast(F32), 0.0).then_inc(s_zero, 1)
            pool.wait_ge(s_zero, 2)
            pipeline(pool, body)

        @block.scalar
        def _(act):
            def copy(out, in_, done):
                nc.scalar.activation(out, in_, ACT.Copy).then_inc(done, 1)

            def body(i, do_a, do_b, do_c, nextA):
                a, b, c = i, i - 1, i - 2
                def gelu(u, bank):
                    act.wait_ge(s_up, UP * c + u + 1)
                    if u == 0:
                        act.wait_ge(s_b1c, c + 1)
                    if u >= 2:
                        act.wait_ge(s_hlo, UP * c + u - 1)
                    else:
                        if later(c):
                            act.wait_ge(s_hlo, UP * c)
                    for k in range(2):
                        f = 2 * u + k
                        ins = nc.scalar.activation(h_in[:, u % 2, k, :], bank[:, k * T:(k + 1) * T],
                                                   ACT.Gelu_apprx_tanh, bias=b1_cur[:, f:f + 1])
                    ins.then_inc(s_hT, 1)

                def place_q(j):
                    rows = slice(RD * j, RD * (j + 1))
                    copy(q_bd[rows, j, :], a1[rows, :], s_qbda)

                def round_w2(u):
                    part = slice(2 * u, 2 * (u + 1))
                    act.wait_ge(s_w2, 16 * (c + 1))
                    if later(c):
                        act.wait_ge(s_yC, c)
                    copy(w2_hi[:, part, :], w2_in[:, part, :], s_w2hi)

                def round_w1(u):
                    part = slice(2 * P * u, 2 * P * (u + 1))
                    act.wait_ge(s_w1, 16 * (b + 1))
                    if do_c:
                        act.wait_ge(s_up, UP * (c + 1))
                    copy(w1_hi[:, :, part], w1_in[:, :, part], s_w1hi)

                if do_a:
                    act.wait_ge(s_qA, a + 1)
                    if later(a):
                        act.wait_ge(s_scA, 4 * a)
                    place_q(0)
                    place_q(1)
                if do_b:
                    act.wait_ge(s_TxB, b + 1)
                    copy(xTB_hi[:, :, :], b0[:, :].rearrange("p (c t) -> p c t", c=C), s_xTB)
                if do_a:
                    place_q(2)
                if do_a:
                    act.wait_ge(s_gA, a + 1)
                    nc.scalar.activation(thA[:, :, :], a0[:, :].rearrange("p (c t) -> p c t", c=C),
                                         ACT.Tanh, scale=0.5).then_inc(s_thA, 1)
                if do_c:
                    round_w2(0)
                    round_w2(1)
                    act.wait_ge(s_TC, c + 1)
                    copy(xTC_hi[:, :, :], c0[:, :].rearrange("p (c t) -> p c t", c=C), s_xTC)
                if do_b:
                    act.wait_ge(s_qB, b + 1)
                    if later(b):
                        act.wait_ge(s_q01, TWO * b)
                    if later(b):
                        act.wait_ge(s_q23, TWO * b)
                    for m in range(C):
                        nc.scalar.activation(q_hi[:, m, :], b0[:, m * T:(m + 1) * T], ACT.Identity,
                                             bias=nbq[:, m:m + 1]).then_inc(s_qhi, 1)
                if do_c:
                    gelu(0, c1)
                    round_w2(2)
                    gelu(1, c0)
                    round_w2(3)
                    gelu(2, c1)
                    gelu(3, c0)
                if do_b:
                    nc.scalar.activation(spare[:, :], minus_half[:, 0:1], ACT.Exp)

                def exps(u):
                    act.wait_ge(s_max, 8 * b + u + 1)
                    if u >= 2 or later(b):
                        act.wait_ge(s_T, 8 * b + u - 1)
                    for g in range(G):
                        ins = nc.scalar.activation(prob[:, u % 2, g, :], S_BANK[u][:, g * P:(g + 1) * P],
                                                   ACT.Exp, bias=negmax[:, u % 2, g:g + 1], scale=-1.0)
                    ins.then_inc(s_prob, 1)

                def probT_even(u):
                    act.wait_ge(s_T, 8 * b + u + 1)
                    if do_c and u == 0:
                        act.wait_ge(s_hlo, UP * (c + 1))
                    if u >= 2 or later(b):
                        act.wait_ge(s_pv, 8 * b + u - 1)
                    copy(probT[:, u % 2, :, :], b1k[:, :].rearrange("p (g n) -> p g n", g=G), s_pTa)

                def context():
                    act.wait_ge(s_TcB, a + 1)
                    copy(cTB_hi[:, :, :], b1k[:, :].rearrange("p (c t) -> p c t", c=C), s_cTB)

                def keys():
                    act.wait_ge(s_kB, a + 1)
                    if later(a):
                        act.wait_ge(s_klo, 2 * a)
                    bank = KEYS_BANK[do_b]
                    for m in range(C):
                        nc.scalar.activation(keys_of(a)[:, m, :], bank[:, m * T:(m + 1) * T],
                                             ACT.Identity, bias=xb_sb[:, 1, m:m + 1]).then_inc(s_kTB, 1)

                def pv_out(seq):
                    act.wait_ge(s_pv, 8 * b + 4 * seq + 4)
                    if seq == 0:
                        if later(b):
                            act.wait_ge(s_K, 2 * b)
                    else:
                        act.wait_ge(s_K, 2 * b + 1)
                    copy(pvT[:, :], b3[:, :], s_pvT)

                if do_b:
                    exps(0)
                if do_a:
                    act.wait_ge(s_ret, a + 1)
                    copy(retT[:, :, :, :], a0[:, :].rearrange("p (c b n) -> p c b n", c=C, b=NB), s_retT)
                if do_b:
                    exps(1)
                    probT_even(0)
                    exps(2)
                if do_a:
                    act.wait_ge(s_rtok, a + 1)
                    nc.scalar.activation(sqA[:, :, :], a1[:, :].rearrange("p (h e) -> p h e", e=RD),
                                         ACT.Square).then_inc(s_sqA, 1)
                if do_a and not do_b:
                    context()
                    keys()
                if do_b:
                    exps(3)
                    probT_even(2)
                    exps(4)
                    exps(5)
                    pv_out(0)
                    probT_even(4)
                    round_w1(0)
                    round_w1(1)
                    exps(6)
                    round_w1(2)
                    exps(7)
                    round_w1(3)
                    probT_even(6)
                if nextA:
                    transposed_x(a + 1)
                if do_b:
                    pv_out(1)
                if do_a and do_b:
                    context()
                if do_b:
                    act.wait_ge(s_aT, b + 1)
                    copy(attT_hi[:, :, :], b2k[:, :].rearrange("p (c t) -> p c t", c=C), s_attT)
                if do_a and do_b:
                    keys()

            def transposed_x(step):
                act.wait_ge(s_TA, step + 1)
                copy(xTA[:, :, :], a0[:, :].rearrange("p (c t) -> p c t", c=C), s_xTA)

            transposed_x(0)
            act.wait_ge(s_wB, 16 * WB_LOADS)
            for n, hi in enumerate((xWq_hi, xWk_hi, xWv_hi, xWo_hi)):
                nc.scalar.activation(hi[:, :, :], xw_in[:, n, :, :], ACT.Copy, scale=-XSCALE if n == 0 else 1.0)\
                    .then_inc(s_xWhi, 1)
            act.wait_ge(s_nbq, 1)
            act.wait_ge(s_const, 9)
            act.wait_ge(s_zerod, 1)
            pipeline(act, body)

        @block.vector
        def _(dve):
            def statistics(step, src, stat, mv, s_ln):
                for b in range(NB):
                    nc.vector.bn_stats(stat[:, b, :], src[:, b, :]).then_inc(s_ln, 1)
                dve.wait_ge(s_ln, 4 * step + 2)
                wait_apart(dve)
                for b in range(NB):
                    ins = nc.vector.bn_aggr(mv[:, b, :], stat[:, b, :])
                ins.then_inc(s_ln, 1)
                dve.wait_ge(s_ln, 4 * step + 3)
                nc.vector.tensor_scalar(mv[:, :, 1], mv[:, :, 1], EPS, None, ALU.add).then_inc(s_ln, 1)

            def normalise(step, src, mv, rs, xn, s_rs, s_xn, s_read):
                dve.wait_ge(s_rs, step + 1)
                if later(step):
                    dve.wait_ge(s_read, step)
                for b in range(NB):
                    nc.vector.tensor_scalar(xn[:, b, :], src[:, b, :], mv[:, b, 0:1], rs[:, b:b + 1],
                                            ALU.subtract, ALU.mult).then_inc(s_xn, 1)

            def split_transposed(s_hi, step, bank, hi, lo, s_lo):
                dve.wait_ge(s_hi, step + 1)
                nc.vector.tensor_tensor(lo[:, :, :], bank[:, :].rearrange("p (c t) -> p c t", c=C),
                                        hi[:, :, :].bitcast(F32), ALU.subtract).then_inc(s_lo, 1)

            def body(i, do_a, do_b, do_c, nextA):
                a, b, c = i, i - 1, i - 2
                def split_masked(h):
                    dve.wait_ge(s_khi, 2 * b + h + 1)
                    nc.vector.scalar_tensor_tensor(out=k_lo[:, h, :, :], in0=keys_of(b)[:, :, :], scalar=head_of[:, h:h + 1],
                                                   in1=k_hi[:, h, :, :].bitcast(F32), op0=ALU.mult,
                                                   op1=ALU.subtract).then_inc(s_klo, 1)

                if do_c:
                    dve.wait_ge(s_x2, c + 1)
                    statistics(c, x2, statC, mvC, s_lnC)
                if do_a:
                    dve.wait_ge(s_qA, a + 1)
                    if later(a):
                        dve.wait_ge(s_scA, 4 * a)
                    rows = slice(RD * (RJ - 1), P)
                    nc.vector.tensor_copy(q_bd[rows, RJ - 1, :], a1[rows, :]).then_inc(s_qbdd, 1)
                if do_b:
                    split_transposed(s_xTB, b, b0, xTB_hi, xTB_lo, s_xTBlo)
                if do_c:
                    normalise(c, x2, mvC, rsC, xnC, s_rsC, s_xnC, s_TC)
                    if later(c):
                        dve.wait_ge(s_hT, UP * c)
                    b1_col = b1T[:, :].rearrange("p (e f) -> p e f", f=FC)
                    nc.vector.tensor_copy(b1_cur[:, :], b1_col[:, c, :]).then_inc(s_b1c, 1)
                if do_b:
                    dve.wait_ge(s_kTB, 2 * (b + 1))
                    if later(b):
                        dve.wait_ge(s_k0, ONE * b)
                    if later(b):
                        dve.wait_ge(s_k1, ONE * b)
                    if later(b):
                        dve.wait_ge(s_k23, TWO * b)
                    for h in range(2):
                        nc.vector.tensor_scalar(k_hi[:, h, :, :], keys_of(b)[:, :, :], head_of[:, h:h + 1], None, ALU.mult)\
                            .then_inc(s_khi, 1)
                    split_masked(0)
                if do_c:
                    split_transposed(s_xTC, c, c0, xTC_hi, xTC_lo, s_xTClo)
                if do_b:
                    split_masked(1)
                if do_a:
                    dve.wait_ge(s_thA, a + 1)
                    if later(a):
                        dve.wait_ge(s_sgA, 2 * a)
                    nc.vector.scalar_tensor_tensor(out=silA[:, :, :], in0=a0[:, :].rearrange("p (c t) -> p c t", c=C),
                                                   scalar=0.0, in1=thA[:, :, :], op0=ALU.add, op1=ALU.mult)\
                        .then_inc(s_silh, 1)
                    dve.wait_ge(s_silh, a + 1)
                    nc.vector.tensor_tensor(silA[:, :, :], a0[:, :].rearrange("p (c t) -> p c t", c=C),
                                            silA[:, :, :], ALU.add).then_inc(s_silA, 1)
                if do_b:
                    dve.wait_ge(s_qhi, 2 * (b + 1))
                    if later(b):
                        dve.wait_ge(s_q01, TWO * b)
                    if later(b):
                        dve.wait_ge(s_q23, TWO * b)
                    for m in range(C):
                        nc.vector.scalar_tensor_tensor(out=q_lo[:, m, :], in0=b0[:, m * T:(m + 1) * T],
                                                       scalar=nbq[:, m:m + 1], in1=q_hi[:, m, :].bitcast(F32),
                                                       op0=ALU.add, op1=ALU.subtract).then_inc(s_qlo, 1)
                if do_a:
                    dve.wait_ge(s_vAp, a + 1)
                    if later(a):
                        dve.wait_ge(s_ret, a)
                    nc.vector.tensor_copy(vA[:, :, :], a1[:, :].rearrange("p (b d) -> p b d", b=NB))\
                        .then_inc(s_vA, 1)
                if do_b:
                    dve.wait_ge(s_vB, b + 1)
                    if later(b):
                        dve.wait_ge(s_pv, 8 * b)
                    nc.vector.tensor_tensor(
                        v_pad[:, :, :, 0:XD], b1k[:, :].rearrange("p (b h e) -> p b h e", b=NB, e=XD),
                        xbv_sb[:, :].rearrange("p (h e) -> p h e", e=XD).unsqueeze(1).broadcast_to([P, NB, XH, XD]),
                        ALU.add).then_inc(s_vpad, 1)

                def decay(u):
                    dve.wait_ge(s_scA, 4 * a + u + 1)
                    if later(a):
                        dve.wait_ge(s_ret, a)
                    bk, cc = u // C, u % C
                    nc.vector.tensor_tensor(scD[:, bk, cc, :, :], SC_BANK[u][:, :].rearrange("p (j n) -> p j n", j=RJ),
                                            decay_sb[:, RJ * cc:RJ * (cc + 1), :], ALU.mult).then_inc(s_scD, 1)

                def split_hidden(u):
                    part = slice(2 * u, 2 * (u + 1))
                    dve.wait_ge(s_hT, UP * c + u + 1)
                    if u == 0:
                        if later(c):
                            dve.wait_ge(s_yC, c)
                    nc.vector.tensor_scalar(h_hi[:, part, :], h_in[:, u % 2, :, :], 1.0, None, ALU.mult)\
                        .then_inc(s_hhi, 1)
                    dve.wait_ge(s_hhi, UP * c + u + 1)
                    nc.vector.tensor_tensor(h_lo[:, part, :], h_in[:, u % 2, :, :],
                                            h_hi[:, part, :].bitcast(F32), ALU.subtract).then_inc(s_hlo, 1)

                def maxima(u):
                    dve.wait_ge(s_S, 8 * b + u + 1)
                    if u >= 2 or later(b):
                        dve.wait_ge(s_prob, 8 * b + u - 1)
                    nc.vector.tensor_reduce(negmax[:, u % 2, :], S_BANK[u][:, :].rearrange("p (g m) -> p g m", g=G),
                                            AX_X, ALU.min).then_inc(s_max, 1)

                def probT_odd(u):
                    dve.wait_ge(s_T, 8 * b + u + 1)
                    if u >= 2 or later(b):
                        dve.wait_ge(s_pv, 8 * b + u - 1)
                    nc.vector.tensor_copy(probT[:, u % 2, :, :],
                                          b1k[:, :].rearrange("p (g n) -> p g n", g=G)).then_inc(s_pTd, 1)

                def divide(seq):
                    dve.wait_ge(s_K, 2 * b + seq + 1)
                    if later(b):
                        dve.wait_ge(s_aT, b)
                    kv = c0[:, :].rearrange("p (h e) -> p h e", e=VP)
                    nc.vector.reciprocal(rden[:, seq, :], kv[:, :, XD]).then_inc(s_rden, 1)
                    dve.wait_ge(s_rden, 2 * b + seq + 1)
                    nc.vector.tensor_tensor(att[:, seq, :, :], kv[:, :, 0:XD],
                                            rden[:, seq, :].unsqueeze(2).broadcast_to([P, XH, XD]), ALU.mult)\
                        .then_inc(s_att, 1)

                if do_a:
                    decay(0)
                    decay(1)
                if do_c:
                    split_hidden(0)
                    split_hidden(1)
                if do_a:
                    decay(2)
                    decay(3)
                if isinstance(i, int) and i == 0:
                    dve.wait_ge(s_xWhi, 4)
                    for n, (hi, lo) in enumerate(((xWq_hi, xWq_lo), (xWk_hi, xWk_lo), (xWv_hi, xWv_lo), (xWo_hi, xWo_lo))):
                        nc.vector.scalar_tensor_tensor(out=lo[:, :, :], in0=xw_in[:, n, :, :],
                                                       scalar=-XSCALE if n == 0 else 1.0,
                                                       in1=hi[:, :, :].bitcast(F32), op0=ALU.mult,
                                                       op1=ALU.subtract).then_inc(s_xWlo, 1)
                if do_b:
                    maxima(0)
                    maxima(1)
                if do_c:
                    split_hidden(2)
                    split_hidden(3)
                if do_b:
                    maxima(2)
                    maxima(3)
                    probT_odd(1)
                if do_a:
                    dve.wait_ge(s_sqA, a + 1)
                    nc.vector.tensor_reduce(varA[:, :], sqA[:, :, :], AX_X, ALU.add).then_inc(s_varA, 1)
                    dve.wait_ge(s_varA, 2 * a + 1)
                    nc.vector.tensor_scalar(varA[:, :], varA[:, :], 1.0 / RD, EPS, ALU.mult, ALU.add)\
                        .then_inc(s_varA, 1)
                if do_a and not do_b:
                    split_transposed(s_cTB, a, b1k, cTB_hi, cTB_lo, s_cTBlo)
                if do_b:
                    maxima(4)
                    maxima(5)
                    probT_odd(3)
                    maxima(6)
                if do_a:
                    dve.wait_ge(s_rstA, a + 1)
                    if later(a):
                        dve.wait_ge(s_rnT, a)
                    nc.vector.tensor_tensor(rnA[:, :, :], a1[:, :].rearrange("p (h e) -> p h e", e=RD),
                                            rstA[:, :].unsqueeze(2).broadcast_to([P, NB * RH, RD]), ALU.mult)\
                        .then_inc(s_rnA, 1)
                if nextA:
                    dve.wait_ge(s_x, 16 * (a + 2))
                    statistics(a + 1, x_in, statA, mvA, s_lnA)
                if do_b:
                    maxima(7)
                if do_a:
                    dve.wait_ge(s_rnT, a + 1)
                    dve.wait_ge(s_sgA, 2 * (a + 1))
                    if later(a):
                        dve.wait_ge(s_yA, a)
                    for k in range(C):
                        nc.vector.scalar_tensor_tensor(out=outT[:, k, :], in0=a0[:, k * T:(k + 1) * T],
                                                       scalar=gn_sb[:, 0, k:k + 1], in1=silA[:, k, :],
                                                       op0=ALU.mult, op1=ALU.add).then_inc(s_outT, 1)
                if do_b:
                    probT_odd(5)
                if nextA:
                    normalise(a + 1, x_in, mvA, rsA, xnA, s_rsA, s_xnA, s_TA)
                if do_a:
                    dve.wait_ge(s_yA, a + 1)
                    dve.wait_ge(s_keep, a + 1)
                    if do_b:
                        dve.wait_ge(s_x1b, b + 1)
                    nc.vector.tensor_tensor(x1[:, :, :], a1[:, :].rearrange("p (b d) -> p b d", b=NB),
                                            x_keep[:, :, :], ALU.add).then_inc(s_x1, 1)
                if do_b:
                    divide(0)
                if do_b:
                    probT_odd(7)
                if do_a:
                    dve.wait_ge(s_x1, a + 1)
                    statistics(a, x1, statB, mvB, s_lnB)
                if do_b:
                    divide(1)
                if do_a and do_b:
                    split_transposed(s_cTB, a, b1k, cTB_hi, cTB_lo, s_cTBlo)
                if do_a:
                    normalise(a, x1, mvB, rsB, xnB, s_rsB, s_xnB, s_TxB)
                if do_b:
                    split_transposed(s_attT, b, b2k, attT_hi, attT_lo, s_attTlo)
                if do_c and not do_b:
                    dve.wait_ge(s_y_half, 1)
                    dve.wait_ge(s_x2b, c + 1)
                    nc.vector.tensor_tensor(x2b[:, 0, :], c1[:, 0:D], x2b[:, 0, :], ALU.add).then_inc(s_yout_half, 1)
                    dve.wait_ge(s_yC, c + 1)
                    nc.vector.tensor_tensor(x2b[:, 1, :], b0[:, 0:D], x2b[:, 1, :], ALU.add).then_inc(s_yout, 1)
                elif do_c:
                    dve.wait_ge(s_yC, c + 1)
                    dve.wait_ge(s_x2b, c + 1)
                    nc.vector.tensor_tensor(x2b[:, :, :], c1[:, :].rearrange("p (b d) -> p b d", b=NB),
                                            x2b[:, :, :], ALU.add).then_inc(s_yout, 1)
                if do_b:
                    dve.wait_ge(s_yB, b + 1)
                    dve.wait_ge(s_x1b, b + 1)
                    if do_c:
                        dve.wait_ge(s_x2b, c + 1)
                    nc.vector.tensor_tensor(x2[:, :, :], b0[:, :].rearrange("p (b d) -> p b d", b=NB),
                                            x1b[:, :, :], ALU.add).then_inc(s_x2, 1)
            dve.wait_ge(s_x, 16)
            statistics(0, x_in, statA, mvA, s_lnA)
            normalise(0, x_in, mvA, rsA, xnA, s_rsA, s_xnA, s_TA)
            dve.wait_ge(s_wH, 16 * WH_LOADS)
            nc.vector.tensor_reduce(wv_mean[:, :], wv_c[:, :, :], AX_X, ALU.add).then_inc(s_cent, 1)
            dve.wait_ge(s_cent, 1)
            nc.vector.tensor_scalar(wv_mean[:, :], wv_mean[:, :], 1.0 / RD, None, ALU.mult).then_inc(s_cent, 1)
            dve.wait_ge(s_cent, 2)
            nc.vector.tensor_tensor(wv_c[:, :, :], wv_c[:, :, :], wv_mean[:, :].unsqueeze(2).broadcast_to([P, C, RD]),
                                    ALU.subtract).then_inc(s_cent, 1)
            for w in (wq_bd, wk_bd, wv_bd):
                nc.vector.memset(w[:, :, :], 0.0).then_inc(s_cent, 1)
            dve.wait_ge(s_cent, 6)
            for w, src in ((wq_bd, wq_c), (wk_bd, wk_c), (wv_bd, wv_c)):
                for j in range(RJ):
                    rows = slice(RD * j, RD * (j + 1))
                    nc.vector.tensor_copy(w[rows, :, rows], src[rows, :, :]).then_inc(s_bd, 1)
            dve.wait_ge(s_wA, 16 * WA_LOADS)
            nc.vector.tensor_scalar(nbq[:, :], xb_sb[:, 0, :], -XSCALE, None, ALU.mult).then_inc(s_nbq, 1)
            dve.wait_ge(s_const, 9)
            nc.vector.tensor_reduce(head_of[:, :], ident[:, :].rearrange("p (r h k) -> p h r k", r=PR, h=2),
                                    AX_XY, ALU.add).then_inc(s_head, 1)
            nc.vector.memset(q_bd[:, :, :], 0.0).then_inc(s_zerod, 1)
            dve.wait_ge(s_setT, 1)
            nc.vector.tensor_copy(wqT_bd[:, :, :], b0[:, 0:D].rearrange("p (c n) -> p c n", c=C))
            nc.vector.tensor_copy(wkT_bd[:, :, :], b0[:, D:2 * D].rearrange("p (c n) -> p c n", c=C))\
                .then_inc(s_setC, 1)
            dve.wait_ge(s_qk, 1)
            nc.vector.tensor_copy(qk_bd[:, :, :], b2k[:, 0:D].rearrange("p (c n) -> p c n", c=C))\
                .then_inc(s_setC, 1)
            dve.wait_ge(s_b1T, 1)
            nc.vector.tensor_copy(b1T[:, :], c0[:, 0:STEPS * FC]).then_inc(s_setC, 1)
            dve.wait_ge(s_zerod, 1)
            dve.wait_ge(s_setC, 3)
            dve.wait_ge(s_head, 1)
            dve.wait_ge(s_nbq, 1)
            pipeline(dve, body)

        @block.tensor
        def _(pe):
            def mm(out, lhsT, rhs, start=True, stop=True):
                return nc.tensor.matmul(out, lhsT, rhs, start=start, stop=stop)

            def mm_split(out, lhsT, rhs, start=True, stop=True):
                if len(rhs) == 1:
                    return mm(out, lhsT[0], rhs[0], start=start, stop=stop)
                mm(out, lhsT[0], rhs[0], start=start, stop=False)
                mm(out, lhsT[0], rhs[1], start=False, stop=False)
                return mm(out, lhsT[1], rhs[0], start=False, stop=stop)

            def transposes(out, src, done):
                for k in range(C):
                    for b in range(NB):
                        col = k * T + b * P
                        ins = nc.tensor.transpose(out[:, col:col + P], src[:, b, k * P:(k + 1) * P], ident[:, :])
                ins.then_inc(done, 1)

            def to_channels(out, w, xT, done):
                for m in range(C):
                    for k in range(C):
                        ins = mm_split(out[:, m * T:(m + 1) * T], [p[:, k, m * P:(m + 1) * P] for p in w],
                                       [p[:, k, :] for p in xT], start=(k == 0), stop=(k == C - 1))
                ins.then_inc(done, 1)

            def to_tokens(out, xT, w, done):
                for b in range(NB):
                    for k in range(C):
                        ins = mm_split(out[:, b * D:(b + 1) * D], [p[:, k, b * P:(b + 1) * P] for p in xT],
                                       [p[:, k, :] for p in w], start=(k == 0), stop=(k == C - 1))
                ins.then_inc(done, 1)

            def body(i, do_a, do_b, do_c, nextA):
                a, b, c = i, i - 1, i - 2

                def ret_scores(u):
                    bk, cc = u // C, u % C
                    if u == 0:
                        pe.wait_ge(s_silA, a + 1)
                    elif u == 1:
                        pe.wait_ge(s_vA, a + 1)
                    else:
                        if u >= 2 or later(a):
                            pe.wait_ge(s_scD, 4 * a + u - 1)
                    tok = slice(bk * P, (bk + 1) * P)
                    qv = q_bd[:, :, :].rearrange("p j (c b n) -> p j c b n", c=C, b=NB)
                    mm(SC_BANK[u][:, :].rearrange("p (j n) -> p j n", j=RJ), xTA[:, cc, tok], qv[:, :, cc, bk, :])\
                        .then_inc(s_scA, 1)

                def scores(u):
                    bk, g = u // 4, GROUP[u % 4]
                    cc, hh = g // 2, g % 2
                    if u == 0:
                        pe.wait_ge(s_q01, TWO * (b + 1))
                        pe.wait_ge(s_k0, ONE * (b + 1))
                        pe.wait_ge(s_k1, ONE * (b + 1))
                    if u == 2:
                        pe.wait_ge(s_q23, TWO * (b + 1))
                        pe.wait_ge(s_k23, TWO * (b + 1))
                    mm(S_BANK[u][:, :], ident_bf[:, :], mask_bf[:, :, :].rearrange("p g m -> p (g m)"),
                       start=True, stop=False)
                    tok = slice(bk * P, (bk + 1) * P)
                    for pair in range(2):
                        r = 2 * hh + pair
                        ins = mm(S_BANK[u][:, pair * 2 * P:(pair + 1) * 2 * P].rearrange("p (h m) -> p h m", h=2),
                                 q_st[:, r, cc, tok], k_st[:, r, :, cc, tok], start=False, stop=(pair == 1))
                    ins.then_inc(s_S, 1)

                def prob_transposes(u):
                    pe.wait_ge(s_prob, 8 * b + u + 1)
                    if u == 0:
                        pe.wait_ge(s_vpad, b + 1)
                    elif u % 2:
                        pe.wait_ge(s_pTa, 4 * b + u // 2 + 1)
                    else:
                        pe.wait_ge(s_pTd, 4 * b + u // 2)
                    for g in range(G):
                        ins = nc.tensor.transpose(b1k[:, g * P:(g + 1) * P], prob[:, u % 2, g, :], ident[:, :])
                    ins.then_inc(s_T, 1)

                def with_values(u):
                    bk, g = u // 4, GROUP[u % 4]
                    if u % 2:
                        pe.wait_ge(s_pTd, 4 * b + u // 2 + 1)
                    else:
                        pe.wait_ge(s_pTa, 4 * b + u // 2 + 1)
                    if u == 0:
                        pe.wait_ge(s_vpad, b + 1)
                        if later(b):
                            pe.wait_ge(s_pvT, 2 * b)
                    if u == 4:
                        pe.wait_ge(s_pvT, 2 * b + 1)
                    for h in range(G):
                        ins = mm(b3[VP * h:VP * (h + 1), g * P:(g + 1) * P], v_pad[:, bk, G * g + h, :],
                                 probT[:, u % 2, h, :])
                    ins.then_inc(s_pv, 1)

                def values_to_tokens(seq):
                    pe.wait_ge(s_pvT, 2 * b + seq + 1)
                    for g in range(4):
                        ins = nc.tensor.transpose(c0[:, g * P:(g + 1) * P], pvT[:, g * P:(g + 1) * P],
                                                  ident[:, :])
                    ins.then_inc(s_K, 1)

                def context():
                    pe.wait_ge(s_c, 16 * (a + 1))
                    if do_b:
                        pe.wait_ge(s_pTd, 4 * (b + 1))
                    transposes(b1k, c_in, s_TcB)

                def keys():
                    pe.wait_ge(s_cTBlo, a + 1)
                    if do_b:
                        pe.wait_ge(s_x1, a + 1)
                    else:
                        pe.wait_ge(s_xWlo, 4)
                    to_channels(KEYS_BANK[do_b], (xWk_hi, xWk_lo), (cTB_hi, cTB_lo), s_kB)

                def up(u, bank):
                    pe.wait_ge(s_w1lo, UP * c + u + 1)
                    for k2 in range(2):
                        f = 2 * u + k2
                        for k in range(C):
                            ins = mm_split(bank[:, k2 * T:(k2 + 1) * T],
                                           [w[:, k, f * P:(f + 1) * P] for w in (w1_hi, w1_lo)],
                                           [t[:, k, :] for t in (xTC_hi, xTC_lo)], start=(k == 0), stop=(k == C - 1))
                    ins.then_inc(s_up, 1)

                def down(piece):
                    bk, quarter = piece // UP, piece % UP
                    if bk == 0:
                        pe.wait_ge(s_hlo, UP * c + quarter + 1)
                        pe.wait_ge(s_w2lo, UP * c + quarter + 1)
                    for f in (2 * quarter, 2 * quarter + 1):
                        ins = mm_split(b0[:, 0:D] if bk and not do_b else c1[:, bk * D:(bk + 1) * D],
                                       [h[:, f, bk * P:(bk + 1) * P] for h in (h_hi, h_lo)],
                                       [w[:, f, :] for w in (w2_hi, w2_lo)], start=(f == 0), stop=(f == FC - 1))
                    if not do_b and piece == UP - 1:
                        ins.then_inc(s_y_half, 1)
                    if piece == NB * UP - 1:
                        ins.then_inc(s_yC, 1)

                if do_a:
                    if later(a):
                        pe.wait_ge(s_x1, a)
                    if later(a):
                        pe.wait_ge(s_kTB, 2 * a)
                    for k in range(C):
                        ins = mm(a1[:, k * T:(k + 1) * T], qk_bd[:, k, :], xTA[:, k, :])
                    ins.then_inc(s_qA, 1)
                    gate(a, 3)
                if do_b:
                    pe.wait_ge(s_xnB, 2 * (b + 1))
                    if later(b):
                        pe.wait_ge(s_x2, b)
                    transposes(b0, xnB, s_TxB)
                    to_tokens(b1k, (cTB_hi, cTB_lo), (xWv_hi, xWv_lo), s_vB)
                if do_a:
                    pe.wait_ge(s_qbda, QJ * (a + 1))
                    pe.wait_ge(s_qbdd, a + 1)
                    for bk in range(NB):
                        for k in range(C):
                            col = bk * D + k * P
                            ins = mm(a1[:, col:col + P], xTA[:, k, bk * P:(bk + 1) * P], wv_bd[:, k, :])
                    ins.then_inc(s_vAp, 1)
                if do_c:
                    pe.wait_ge(s_xnC, 2 * (c + 1))
                    pe.wait_ge(s_att, 2 * (c + 1))
                    transposes(c0, xnC, s_TC)
                if do_b:
                    pe.wait_ge(s_xTBlo, b + 1)
                    to_channels(b0, (xWq_hi, xWq_lo), (xTB_hi, xTB_lo), s_qB)
                if do_c:
                    pe.wait_ge(s_xTClo, c + 1)
                    if later(c):
                        pe.wait_ge(s_yout, c)
                    up(0, c1)
                    up(1, c0)
                if do_a:
                    ret_scores(0)
                    ret_scores(1)
                if do_c:
                    pe.wait_ge(s_hT, UP * c + 1)
                    up(2, c1)
                    pe.wait_ge(s_hT, UP * c + 2)
                    up(3, c0)
                if do_a:
                    ret_scores(2)
                    ret_scores(3)
                if do_b:
                    scores(0)
                    scores(1)
                if do_a:
                    pe.wait_ge(s_scD, 4 * (a + 1))
                    for cc in range(C):
                        for bk in range(NB):
                            for j in range(RJ):
                                h = RJ * cc + j
                                ins = mm(a0[RD * j:RD * (j + 1), cc * T + bk * P:cc * T + (bk + 1) * P],
                                         vA[:, bk, RD * h:RD * (h + 1)], scD[:, bk, cc, j, :])
                    ins.then_inc(s_ret, 1)
                if do_b and do_c:
                    pe.wait_ge(s_hT, UP * (c + 1))
                elif do_c:
                    pe.wait_ge(s_hT, UP * c + UP - 1)
                if do_b:
                    scores(2)
                if do_c:
                    down(0)
                    down(1)
                if do_b:
                    prob_transposes(0)
                    scores(3)
                if do_a:
                    pe.wait_ge(s_retT, a + 1)
                    for bk in range(NB):
                        for cc in range(C):
                            col = bk * D + cc * P
                            ins = nc.tensor.transpose(a1[:, col:col + P], retT[:, cc, bk, :], ident[:, :])
                    ins.then_inc(s_rtok, 1)
                if do_a and not do_b:
                    context()
                    keys()
                if do_b:
                    prob_transposes(1)
                    scores(4)
                    with_values(0)
                if do_c:
                    down(2)
                if do_b:
                    prob_transposes(2)
                    scores(5)
                    with_values(1)
                if do_c:
                    down(3)
                if do_b:
                    prob_transposes(3)
                    scores(6)
                    with_values(2)
                if do_c:
                    down(4)
                if do_b:
                    with_values(3)
                    prob_transposes(4)
                    scores(7)
                if do_c:
                    down(5)
                if do_b:
                    prob_transposes(5)
                if do_a:
                    pe.wait_ge(s_rnA, a + 1)
                    for k in range(C):
                        for bk in range(NB):
                            col = k * T + bk * P
                            src = rnA[:, :, :].rearrange("p (b h) e -> p b (h e)", b=NB)
                            ins = nc.tensor.transpose(a0[:, col:col + P], src[:, bk, k * P:(k + 1) * P], ident[:, :])
                    ins.then_inc(s_rnT, 1)
                if do_b:
                    values_to_tokens(0)
                    with_values(4)
                if do_c:
                    down(6)
                if do_a:
                    pe.wait_ge(s_outT, 2 * (a + 1))
                    to_tokens(a1, (outT,), (W2_sb,), s_yA)
                if do_b:
                    prob_transposes(6)
                    with_values(5)
                if nextA:
                    transposed_x(a + 1)
                if do_b:
                    prob_transposes(7)
                    with_values(6)
                if do_c:
                    down(7)
                if do_b:
                    with_values(7)
                if do_a and do_b:
                    context()
                if nextA:
                    gate(a + 1, 0)
                if do_b:
                    pe.wait_ge(s_att, 2 * b + 1)
                    values_to_tokens(1)
                if nextA:
                    gate(a + 1, 1)
                    gate(a + 1, 2)
                if do_b:
                    pe.wait_ge(s_att, 2 * (b + 1))
                    attv = att[:, :, :, :].rearrange("p b h e -> p b (h e)")
                    transposes(b2k, attv, s_aT)
                if do_a and do_b:
                    keys()
                if do_b:
                    pe.wait_ge(s_attTlo, b + 1)
                    to_tokens(b0, (attT_hi, attT_lo), (xWo_hi, xWo_lo), s_yB)

            def transposed_x(step):
                pe.wait_ge(s_xnA, 2 * (step + 1))
                if later(step):
                    pe.wait_ge(s_outT, 2 * step)
                transposes(a0, xnA, s_TA)

            def gate(step, piece):
                m, k = piece // C, piece % C
                if piece == 0:
                    pe.wait_ge(s_xTA, step + 1)
                ins = mm(a0[:, m * T:(m + 1) * T], W1_sb[:, k, m * P:(m + 1) * P], xTA[:, k, :],
                         start=(k == 0), stop=(k == C - 1))
                if piece == C * C - 1:
                    ins.then_inc(s_gA, 1)

            pe.wait_ge(s_const, 9)
            transposed_x(0)
            pe.wait_ge(s_wA, 16 * WA_LOADS)
            for n in range(3):
                gate(0, n)
            pe.wait_ge(s_bd, 3 * RJ)
            for n, w in enumerate((wq_bd, wk_bd)):
                for k in range(C):
                    ins = nc.tensor.transpose(b0[:, (C * n + k) * P:(C * n + k + 1) * P], w[:, k, :], ident[:, :])
            ins.then_inc(s_setT, 1)
            pe.wait_ge(s_setC, 1)
            for k in range(C):
                ins = mm(b2k[:, k * P:(k + 1) * P], wqT_bd[:, k, :], wkT_bd[:, k, :])
            ins.then_inc(s_qk, 1)
            pe.wait_ge(s_wB, 16 * WB_LOADS)
            n = STEPS * FC
            nc.tensor.transpose(c0[:, 0:n], b1_rows[:, :], ident[0:n, 0:n]).then_inc(s_b1T, 1)
            pe.wait_ge(s_setC, 3)
            pipeline(pe, body)


_INS = ['x', 'ctx_1024', 'L0_attn_Wq', 'L0_attn_Wk', 'L0_attn_Wv', 'L0_attn_W1', 'L0_attn_W2', 'L0_attn_gn_w',
        'L0_attn_gn_b', 'L0_xattn_Wq', 'L0_xattn_bq', 'L0_xattn_Wk', 'L0_xattn_bk', 'L0_xattn_Wv', 'L0_xattn_bv',
        'L0_xattn_Wo', 'L0_xattn_bo', 'L0_ffn_w1', 'L0_ffn_b1', 'L0_ffn_w2', 'L0_ffn_b2']


def kernel(**inputs):
    import concourse.bacc as bacc
    from concourse.bass_utils import run_bass_kernel_spmd

    nc = bacc.Bacc("TRN2", target_bir_lowering=False, num_devices=1)
    arrays, args = {}, []
    for name in _INS:
        arrays[f"in_{name}"] = np.ascontiguousarray(inputs[name])
    arrays["in_decay"] = decay_table()
    for name, a in arrays.items():
        args.append(nc.dram_tensor(name, a.shape, mybir.dt.from_np(a.dtype), kind="ExternalInput").ap())
    out = nc.dram_tensor("out", (STEPS * NB, P, D), F32, kind="ExternalOutput").ap()
    decoder_kernel(nc, *args, out)
    r = run_bass_kernel_spmd(nc, [arrays], core_ids=[0])
    return r.results[0]["out"]
```
